# Optimizing a Trainium2 kernel written in Bass

```python
import numpy as np
import jax
import jax.numpy as jnp

def _softmax(x, axis=-1):
    return jax.nn.softmax(x, axis=axis)

def _gelu(x):
    return jax.nn.gelu(x, approximate=True)

def _silu(x):
    return jax.nn.silu(x)

def _sigmoid(x):
    return jax.nn.sigmoid(x)

def _layernorm(x, axis=-1, eps=1e-05):
    m = jnp.mean(x, axis=axis, keepdims=True)
    v = jnp.var(x, axis=axis, keepdims=True)
    return (x - m) / jnp.sqrt(v + eps)

def _scatter_add(tgt, idx, src, axis=0):
    return tgt.at[idx].add(src)

def _segment_sum(src, seg, n):
    return jax.ops.segment_sum(src, seg, n)
kernel_name = 'mk_xattn_seq_d4_seqx_r8_47f2be'

def setup_inputs(seed: int=0):
    np.random.seed(seed)
    _w = jnp.asarray

    def _rec_inputs():
        import jax
        import jax.numpy as jnp
        _rk = jax.random.key(seed)
        x = -1.394e-06 + 0.9999 * jax.random.normal(jax.random.fold_in(_rk, 1), (4, 256, 128), jnp.float32)
        _lenS = 256 - jax.random.randint(jax.random.fold_in(_rk, 7), (4,), 0, max(1, 256 // 4) + 1, jnp.int32)
        _lenS2 = 256 - jax.random.randint(jax.random.fold_in(_rk, 8), (4,), 0, max(1, 256 // 4) + 1, jnp.int32)
        _ctx_512P = jax.random.normal(jax.random.fold_in(_rk, 11), (4, 16, 64), jnp.float32)
        _ctx_512c = jax.random.dirichlet(jax.random.fold_in(_rk, 511), 0.3 * jnp.ones((16,), jnp.float32), (4, 256))
        _ctx_512t = jnp.einsum('bsk,bkd->bsd', _ctx_512c, _ctx_512P)
        _ctx_512t = _ctx_512t * jax.lax.rsqrt(jnp.mean(jnp.square(_ctx_512t)) + 1e-12) * 0.953939
        ctx_512 = -0.00065366 + 1.00074 * (_ctx_512t + 0.3 * jax.random.normal(jax.random.fold_in(_rk, 611), (4, 256, 64), jnp.float32))
        _validS = jnp.arange(256)[None, :] < _lenS[:, None]
        _validS2 = jnp.arange(256)[None, :] < _lenS2[:, None]
        _causal = jnp.tril(jnp.ones((256, 256), dtype=bool))
        mask_BxSxS_ik0 = jnp.where(jnp.broadcast_to(_validS[:, None, :], (4, 256, 256)), 0, 1).astype(jnp.int32)
        mask_Bx1xS2_if1 = jnp.where(jnp.ones((4, 1, 256), dtype=bool), 1, 0).astype(jnp.int32)
        return (x, ctx_512, mask_BxSxS_ik0, mask_Bx1xS2_if1)
    x, ctx_512, mask_BxSxS_ik0, mask_Bx1xS2_if1 = _rec_inputs()

    def _L0_xattn_setup():
        import jax, jax.numpy as jnp
        import numpy as np
        B, ST, SS = (8, 64, 72)
        TD, SD = (128, 64)
        L, H, D, FF = (6, 16, 64, 512)

        def _ln(x, g, b, eps=1e-05):
            m = jnp.mean(x, axis=-1, keepdims=True)
            v = jnp.mean(jnp.square(x - m), axis=-1, keepdims=True)
            return (x - m) / jnp.sqrt(v + eps) * g + b

        def _heads(x):
            b, s, _ = x.shape
            return x.reshape(b, s, H, D).transpose(0, 2, 1, 3)

        def _mha(s, t, kv_w, q_w, o_w, o_b, mask):
            kv = s @ kv_w
            k, v = jnp.split(kv, 2, axis=-1)
            q = t @ q_w
            k, v, q = (_heads(k), _heads(v), _heads(q))
            scores = jnp.einsum('bhqd,bhkd->bhqk', q, k) * D ** (-0.5)
            scores = jnp.where(mask[:, None] == 0, jnp.float32(-1000000000.0), scores)
            attn = jax.nn.softmax(scores, axis=-1)
            o = jnp.einsum('bhqk,bhkd->bhqd', attn, v)
            o = o.transpose(0, 2, 1, 3).reshape(t.shape[0], t.shape[1], H * D)
            return o @ o_w + o_b
        key = jax.random.key(seed)
        ks = jax.random.split(key, 18)
        sc = 0.02
        inp = {'src': jax.random.normal(ks[0], (B, SS, SD), jnp.float32), 'tgt': jax.random.normal(ks[1], (B, ST, TD), jnp.float32), 'tgt_mask': jnp.broadcast_to(jnp.tril(jnp.ones((ST, ST), jnp.int32)), (B, ST, ST)), 'src_mask': jnp.ones((B, 1, SS), jnp.int32), 'norm_g': jnp.ones((TD,), jnp.float32), 'norm_b': jnp.zeros((TD,), jnp.float32), 'sa_kv': jax.random.normal(ks[2], (L, TD, 2 * H * D), jnp.float32) * sc, 'sa_q': jax.random.normal(ks[3], (L, TD, H * D), jnp.float32) * sc, 'sa_ow': jax.random.normal(ks[4], (L, H * D, TD), jnp.float32) * sc, 'sa_ob': jnp.zeros((L, TD), jnp.float32), 'ca_kv': jax.random.normal(ks[5], (L, SD, 2 * H * D), jnp.float32) * sc, 'ca_q': jax.random.normal(ks[6], (L, TD, H * D), jnp.float32) * sc, 'ca_ow': jax.random.normal(ks[7], (L, H * D, TD), jnp.float32) * sc, 'ca_ob': jnp.zeros((L, TD), jnp.float32), 'ff_w1': jax.random.normal(ks[8], (L, TD, FF), jnp.float32) * sc, 'ff_b1': jnp.zeros((L, FF), jnp.float32), 'ff_w2': jax.random.normal(ks[9], (L, FF, TD), jnp.float32) * sc, 'ff_b2': jnp.zeros((L, TD), jnp.float32), 'pre_g': jnp.ones((L, TD), jnp.float32), 'pre_b': jnp.zeros((L, TD), jnp.float32)}
        return inp
    _L0_xattn_all = _L0_xattn_setup()
    _L0_xattn_in = {k: v for k, v in _L0_xattn_all.items() if k in ('norm_g', 'norm_b', 'sa_kv', 'sa_q', 'sa_ow', 'sa_ob', 'ca_kv', 'ca_q', 'ca_ow', 'ca_ob', 'ff_w1', 'ff_b1', 'ff_w2', 'ff_b2', 'pre_g', 'pre_b')}
    del _L0_xattn_all

    def _L1_xattn_setup():
        import jax, jax.numpy as jnp
        import numpy as np
        QUERY_DIM = 128
        KEY_DIM = 64
        HIDDEN_DIM = 128
        B, LQ, LK = (8, 256, 256)
        key = jax.random.key(seed)
        ks = jax.random.split(key, 10)
        s_q = 1.0 / np.sqrt(QUERY_DIM)
        s_k = 1.0 / np.sqrt(KEY_DIM)
        s_h = 1.0 / np.sqrt(HIDDEN_DIM)
        return {'query': jax.random.normal(ks[0], (B, LQ, QUERY_DIM), jnp.float32), 'key': jax.random.normal(ks[1], (B, LK, KEY_DIM), jnp.float32), 'Wq': jax.random.uniform(ks[2], (QUERY_DIM, HIDDEN_DIM), jnp.float32, -s_q, s_q), 'bq': jax.random.uniform(ks[3], (HIDDEN_DIM,), jnp.float32, -s_q, s_q), 'Wk': jax.random.uniform(ks[4], (KEY_DIM, HIDDEN_DIM), jnp.float32, -s_k, s_k), 'bk': jax.random.uniform(ks[5], (HIDDEN_DIM,), jnp.float32, -s_k, s_k), 'Wv': jax.random.uniform(ks[6], (KEY_DIM, HIDDEN_DIM), jnp.float32, -s_k, s_k), 'bv': jax.random.uniform(ks[7], (HIDDEN_DIM,), jnp.float32, -s_k, s_k), 'Wo': jax.random.uniform(ks[8], (HIDDEN_DIM, QUERY_DIM), jnp.float32, -s_h, s_h), 'bo': jax.random.uniform(ks[9], (QUERY_DIM,), jnp.float32, -s_h, s_h)}
    _L1_xattn_all = _L1_xattn_setup()
    _L1_xattn_in = {k: v for k, v in _L1_xattn_all.items() if k in ('Wq', 'bq', 'Wk', 'bk', 'Wv', 'bv', 'Wo', 'bo')}
    del _L1_xattn_all

    def _L2_xattn_setup():
        import jax, jax.numpy as jnp
        import numpy as np
        B, T, E = (8, 512, 128)
        M, L = (32, 64)
        EPS = 1e-06
        key = jax.random.key(seed)
        ks = jax.random.split(key, 5)
        return {'emb': jax.random.normal(ks[0], (B, T, E), dtype=jnp.float32), 'latent': jax.random.normal(ks[1], (B, M, L), dtype=jnp.float32), 'Wq': jax.random.normal(ks[2], (E, E), dtype=jnp.float32) * (1.0 / np.sqrt(E)), 'bq': jnp.zeros((E,), dtype=jnp.float32), 'Wk': jax.random.normal(ks[3], (L, E), dtype=jnp.float32) * (1.0 / np.sqrt(L)), 'bk': jnp.zeros((E,), dtype=jnp.float32), 'Wv': jax.random.normal(ks[4], (L, E), dtype=jnp.float32) * (1.0 / np.sqrt(L)), 'bv': jnp.zeros((E,), dtype=jnp.float32), 'gamma': jnp.ones((E,), dtype=jnp.float32), 'beta': jnp.zeros((E,), dtype=jnp.float32)}
    _L2_xattn_all = _L2_xattn_setup()
    _L2_xattn_in = {k: v for k, v in _L2_xattn_all.items() if k in ('Wq', 'bq', 'Wk', 'bk', 'Wv', 'bv', 'gamma', 'beta')}
    del _L2_xattn_all

    def _L3_xattn_setup():
        import jax, jax.numpy as jnp
        import numpy as np
        QUERY_DIM = 128
        KEY_DIM = 64
        HIDDEN_DIM = 128
        B, LQ, LK = (8, 256, 256)
        key = jax.random.key(seed)
        ks = jax.random.split(key, 10)
        s_q = 1.0 / np.sqrt(QUERY_DIM)
        s_k = 1.0 / np.sqrt(KEY_DIM)
        s_h = 1.0 / np.sqrt(HIDDEN_DIM)
        return {'query': jax.random.normal(ks[0], (B, LQ, QUERY_DIM), jnp.float32), 'key': jax.random.normal(ks[1], (B, LK, KEY_DIM), jnp.float32), 'Wq': jax.random.uniform(ks[2], (QUERY_DIM, HIDDEN_DIM), jnp.float32, -s_q, s_q), 'bq': jax.random.uniform(ks[3], (HIDDEN_DIM,), jnp.float32, -s_q, s_q), 'Wk': jax.random.uniform(ks[4], (KEY_DIM, HIDDEN_DIM), jnp.float32, -s_k, s_k), 'bk': jax.random.uniform(ks[5], (HIDDEN_DIM,), jnp.float32, -s_k, s_k), 'Wv': jax.random.uniform(ks[6], (KEY_DIM, HIDDEN_DIM), jnp.float32, -s_k, s_k), 'bv': jax.random.uniform(ks[7], (HIDDEN_DIM,), jnp.float32, -s_k, s_k), 'Wo': jax.random.uniform(ks[8], (HIDDEN_DIM, QUERY_DIM), jnp.float32, -s_h, s_h), 'bo': jax.random.uniform(ks[9], (QUERY_DIM,), jnp.float32, -s_h, s_h)}
    _L3_xattn_all = _L3_xattn_setup()
    _L3_xattn_in = {k: v for k, v in _L3_xattn_all.items() if k in ('Wq', 'bq', 'Wk', 'bk', 'Wv', 'bv', 'Wo', 'bo')}
    del _L3_xattn_all
    return {'x': x, 'ctx_512': ctx_512, 'mask_BxSxS_ik0': mask_BxSxS_ik0, 'mask_Bx1xS2_if1': mask_Bx1xS2_if1, 'L0_xattn_norm_g': _L0_xattn_in['norm_g'], 'L0_xattn_norm_b': _L0_xattn_in['norm_b'], 'L0_xattn_sa_kv': _L0_xattn_in['sa_kv'], 'L0_xattn_sa_q': _L0_xattn_in['sa_q'], 'L0_xattn_sa_ow': _L0_xattn_in['sa_ow'], 'L0_xattn_sa_ob': _L0_xattn_in['sa_ob'], 'L0_xattn_ca_kv': _L0_xattn_in['ca_kv'], 'L0_xattn_ca_q': _L0_xattn_in['ca_q'], 'L0_xattn_ca_ow': _L0_xattn_in['ca_ow'], 'L0_xattn_ca_ob': _L0_xattn_in['ca_ob'], 'L0_xattn_ff_w1': _L0_xattn_in['ff_w1'], 'L0_xattn_ff_b1': _L0_xattn_in['ff_b1'], 'L0_xattn_ff_w2': _L0_xattn_in['ff_w2'], 'L0_xattn_ff_b2': _L0_xattn_in['ff_b2'], 'L0_xattn_pre_g': _L0_xattn_in['pre_g'], 'L0_xattn_pre_b': _L0_xattn_in['pre_b'], 'L1_xattn_Wq': _L1_xattn_in['Wq'], 'L1_xattn_bq': _L1_xattn_in['bq'], 'L1_xattn_Wk': _L1_xattn_in['Wk'], 'L1_xattn_bk': _L1_xattn_in['bk'], 'L1_xattn_Wv': _L1_xattn_in['Wv'], 'L1_xattn_bv': _L1_xattn_in['bv'], 'L1_xattn_Wo': _L1_xattn_in['Wo'], 'L1_xattn_bo': _L1_xattn_in['bo'], 'L2_xattn_Wq': _L2_xattn_in['Wq'], 'L2_xattn_bq': _L2_xattn_in['bq'], 'L2_xattn_Wk': _L2_xattn_in['Wk'], 'L2_xattn_bk': _L2_xattn_in['bk'], 'L2_xattn_Wv': _L2_xattn_in['Wv'], 'L2_xattn_bv': _L2_xattn_in['bv'], 'L2_xattn_gamma': _L2_xattn_in['gamma'], 'L2_xattn_beta': _L2_xattn_in['beta'], 'L3_xattn_Wq': _L3_xattn_in['Wq'], 'L3_xattn_bq': _L3_xattn_in['bq'], 'L3_xattn_Wk': _L3_xattn_in['Wk'], 'L3_xattn_bk': _L3_xattn_in['bk'], 'L3_xattn_Wv': _L3_xattn_in['Wv'], 'L3_xattn_bv': _L3_xattn_in['bv'], 'L3_xattn_Wo': _L3_xattn_in['Wo'], 'L3_xattn_bo': _L3_xattn_in['bo']}

def reference(x, ctx_512, mask_BxSxS_ik0, mask_Bx1xS2_if1, L0_xattn_norm_g, L0_xattn_norm_b, L0_xattn_sa_kv, L0_xattn_sa_q, L0_xattn_sa_ow, L0_xattn_sa_ob, L0_xattn_ca_kv, L0_xattn_ca_q, L0_xattn_ca_ow, L0_xattn_ca_ob, L0_xattn_ff_w1, L0_xattn_ff_b1, L0_xattn_ff_w2, L0_xattn_ff_b2, L0_xattn_pre_g, L0_xattn_pre_b, L1_xattn_Wq, L1_xattn_bq, L1_xattn_Wk, L1_xattn_bk, L1_xattn_Wv, L1_xattn_bv, L1_xattn_Wo, L1_xattn_bo, L2_xattn_Wq, L2_xattn_bq, L2_xattn_Wk, L2_xattn_bk, L2_xattn_Wv, L2_xattn_bv, L2_xattn_gamma, L2_xattn_beta, L3_xattn_Wq, L3_xattn_bq, L3_xattn_Wk, L3_xattn_bk, L3_xattn_Wv, L3_xattn_bv, L3_xattn_Wo, L3_xattn_bo):
    import jax
    import jax.numpy as jnp

    def _L0_xattn_ref(src, tgt, tgt_mask, src_mask, norm_g, norm_b, sa_kv, sa_q, sa_ow, sa_ob, ca_kv, ca_q, ca_ow, ca_ob, ff_w1, ff_b1, ff_w2, ff_b2, pre_g, pre_b):
        import jax, jax.numpy as jnp
        import numpy as np
        B, ST, SS = (8, 64, 72)
        TD, SD = (128, 64)
        L, H, D, FF = (6, 16, 64, 512)

        def _ln(x, g, b, eps=1e-05):
            m = jnp.mean(x, axis=-1, keepdims=True)
            v = jnp.mean(jnp.square(x - m), axis=-1, keepdims=True)
            return (x - m) / jnp.sqrt(v + eps) * g + b

        def _heads(x):
            b, s, _ = x.shape
            return x.reshape(b, s, H, D).transpose(0, 2, 1, 3)

        def _mha(s, t, kv_w, q_w, o_w, o_b, mask):
            kv = s @ kv_w
            k, v = jnp.split(kv, 2, axis=-1)
            q = t @ q_w
            k, v, q = (_heads(k), _heads(v), _heads(q))
            scores = jnp.einsum('bhqd,bhkd->bhqk', q, k) * D ** (-0.5)
            scores = jnp.where(mask[:, None] == 0, jnp.float32(-1000000000.0), scores)
            attn = jax.nn.softmax(scores, axis=-1)
            o = jnp.einsum('bhqk,bhkd->bhqd', attn, v)
            o = o.transpose(0, 2, 1, 3).reshape(t.shape[0], t.shape[1], H * D)
            return o @ o_w + o_b
        stacked = (sa_kv, sa_q, sa_ow, sa_ob, ca_kv, ca_q, ca_ow, ca_ob, ff_w1, ff_b1, ff_w2, ff_b2, pre_g, pre_b)

        def step(t, p):
            skv, sq, sow, sob, ckv, cq, cow, cob, w1, b1, w2, b2, pg, pb = p
            tn = _ln(t, norm_g, norm_b)
            t = _mha(tn, tn, skv, sq, sow, sob, tgt_mask) + t
            tn = _ln(t, norm_g, norm_b)
            t = _mha(src, tn, ckv, cq, cow, cob, src_mask) + t
            tn = _ln(t, pg, pb)
            t = t + (jax.nn.relu(tn @ w1 + b1) @ w2 + b2)
            return (t, None)
        out, _ = jax.lax.scan(step, tgt, stacked)
        return out

    def _L1_xattn_ref(query, key, Wq, bq, Wk, bk, Wv, bv, Wo, bo):
        import jax, jax.numpy as jnp
        import numpy as np
        QUERY_DIM = 128
        KEY_DIM = 64
        HIDDEN_DIM = 128
        B, LQ, LK = (8, 256, 256)
        scale = HIDDEN_DIM ** (-0.5)
        Q = jnp.einsum('bqd,dh->bqh', query, Wq) + bq
        K = jnp.einsum('bkd,dh->bkh', key, Wk) + bk
        V = jnp.einsum('bkd,dh->bkh', key, Wv) + bv
        scores = jnp.einsum('bqh,bkh->bqk', Q, K) * scale
        weights = jax.nn.softmax(scores, axis=-1)
        attended = jnp.einsum('bqk,bkh->bqh', weights, V)
        out = jnp.einsum('bqh,hd->bqd', attended, Wo) + bo
        return query + out

    def _L2_xattn_ref(emb, latent, Wq, bq, Wk, bk, Wv, bv, gamma, beta):
        import jax, jax.numpy as jnp
        import numpy as np
        B, T, E = (8, 512, 128)
        M, L = (32, 64)
        EPS = 1e-06
        q = jnp.einsum('bte,ef->btf', emb, Wq) + bq
        k = jnp.einsum('bml,le->bme', latent, Wk) + bk
        v = jnp.einsum('bml,le->bme', latent, Wv) + bv
        scale = 1.0 / jnp.sqrt(jnp.asarray(E, dtype=q.dtype))
        w = jnp.einsum('bte,bme->btm', q, k) * scale
        w = jax.nn.softmax(w, axis=1)
        pred = jnp.einsum('btm,bme->bte', w, v)
        x = pred + emb
        mu = jnp.mean(x, axis=-1, keepdims=True)
        var = jnp.var(x, axis=-1, keepdims=True)
        return (x - mu) * jax.lax.rsqrt(var + EPS) * gamma + beta

    def _L3_xattn_ref(query, key, Wq, bq, Wk, bk, Wv, bv, Wo, bo):
        import jax, jax.numpy as jnp
        import numpy as np
        QUERY_DIM = 128
        KEY_DIM = 64
        HIDDEN_DIM = 128
        B, LQ, LK = (8, 256, 256)
        scale = HIDDEN_DIM ** (-0.5)
        Q = jnp.einsum('bqd,dh->bqh', query, Wq) + bq
        K = jnp.einsum('bkd,dh->bkh', key, Wk) + bk
        V = jnp.einsum('bkd,dh->bkh', key, Wv) + bv
        scores = jnp.einsum('bqh,bkh->bqk', Q, K) * scale
        weights = jax.nn.softmax(scores, axis=-1)
        attended = jnp.einsum('bqk,bkh->bqh', weights, V)
        out = jnp.einsum('bqh,hd->bqd', attended, Wo) + bo
        return query + out
    x = _L0_xattn_ref(ctx_512, x, mask_BxSxS_ik0, mask_Bx1xS2_if1, L0_xattn_norm_g, L0_xattn_norm_b, L0_xattn_sa_kv, L0_xattn_sa_q, L0_xattn_sa_ow, L0_xattn_sa_ob, L0_xattn_ca_kv, L0_xattn_ca_q, L0_xattn_ca_ow, L0_xattn_ca_ob, L0_xattn_ff_w1, L0_xattn_ff_b1, L0_xattn_ff_w2, L0_xattn_ff_b2, L0_xattn_pre_g, L0_xattn_pre_b)
    x = _L1_xattn_ref(x, ctx_512, L1_xattn_Wq, L1_xattn_bq, L1_xattn_Wk, L1_xattn_bk, L1_xattn_Wv, L1_xattn_bv, L1_xattn_Wo, L1_xattn_bo)
    x = _L2_xattn_ref(x, ctx_512, L2_xattn_Wq, L2_xattn_bq, L2_xattn_Wk, L2_xattn_bk, L2_xattn_Wv, L2_xattn_bv, L2_xattn_gamma, L2_xattn_beta)
    x = _L3_xattn_ref(x, ctx_512, L3_xattn_Wq, L3_xattn_bq, L3_xattn_Wk, L3_xattn_bk, L3_xattn_Wv, L3_xattn_bv, L3_xattn_Wo, L3_xattn_bo)
    return x

_drawn_inputs = setup_inputs


def setup_inputs(seed=0):
    import zlib

    import numpy as np

    out = dict(_drawn_inputs(seed))
    spreads = {'L0_xattn_norm_g': (1.0, 0.6),
     'L0_xattn_norm_b': (0.0, 0.1),
     'L0_xattn_sa_ob': (0.0, 0.1),
     'L0_xattn_ca_ob': (0.0, 0.1),
     'L0_xattn_ff_b1': (0.0, 0.1),
     'L0_xattn_ff_b2': (0.0, 0.1),
     'L0_xattn_pre_g': (1.0, 0.537),
     'L0_xattn_pre_b': (0.0, 0.576),
     'L2_xattn_bq': (0.0, 2.0),
     'L2_xattn_bk': (0.0, 0.1),
     'L2_xattn_bv': (0.0, 0.1),
     'L2_xattn_gamma': (1.0, 0.2),
     'L2_xattn_beta': (0.0, 0.1)}
    factors = {'L0_xattn_sa_q': 8.0,
     'L0_xattn_ca_q': 27.47,
     'L1_xattn_Wq': 2.858,
     'L1_xattn_bq': 8.0,
     'L1_xattn_Wk': 2.914,
     'L1_xattn_bk': 64.0,
     'L3_xattn_bq': 35.353,
     'L3_xattn_bk': 64.0}
    for name, (base, spread) in spreads.items():
        noise = np.random.default_rng([zlib.crc32(name.encode()), seed]).standard_normal(out[name].shape)
        drawn = base * np.exp(spread * noise) if base else spread * noise
        out[name] = jnp.asarray(drawn.astype(out[name].dtype))
    for name, factor in factors.items():
        out[name] = (out[name] * factor).astype(out[name].dtype)
    return out
```

```python
from contextlib import ExitStack

import concourse.bass as bass
from concourse import mybir

F32 = mybir.dt.float32
I32 = mybir.dt.int32
ALU = mybir.AluOpType
ACT = mybir.ActivationFunctionType

B, S, TD, SD = 4, 256, 128, 64
LAYERS, H, D, FF = 6, 16, 64, 512
P = 128
RT = S // P
PAIRS = H // 2
SELF = B * PAIRS
STEPS = 2 * SELF
CUT = PAIRS
MASKED = -float(2 ** 100)
EPS, EPS2 = 1e-5, 1e-6
SCALE = D ** -0.5
SCALE1 = TD ** -0.5

RESIDUAL = ("self_out", "cross_out", "mlp_down")


def body_fillers():
    out = []
    for b in range(B):
        nxt = STEPS if b < 2 else 0
        first = {0: 47, 1: 55, 2: 8, 3: 16}[b]
        start = nxt + PAIRS * b
        for c in range(PAIRS // 2):
            for kind in ("q", "k"):
                out.append((kind, b, c, first, start - 2 + 2 * c))
        for c in range(2 * RT):
            out.append(("v", b, c, first, start - 1))
        out.append(("self_out", b, 0, PAIRS * (b + 1), PAIRS * (b + 1) + 2))
        out.append(("norm_cross", b, 0, ("after", "self_out", 2), PAIRS * (b + 1) + 5))
        for c in range(PAIRS // 2):
            out.append(("cq", b, c, max(PAIRS * (b + 1) + 4, SELF + PAIRS * (b - 1)), SELF + PAIRS * b - 2 + 2 * c))
        end = SELF + PAIRS * (b + 1)
        out.append(("cross_out", b, 0, end, end + 1))
        out.append(("norm_mlp", b, 0, ("after", "cross_out", 2), end + 3))
        for c in range(2):
            out.append(("mlp_up", b, c, ("after", "norm_mlp", 1), end + 4))
        out.append(("mlp_down", b, 0, ("after", "mlp_up", 1), end + 5))
        out.append(("norm_self", b, 0, ("after", "mlp_down", 2), end + 7))
    for c in range(2):
        out.append(("fold_q", 0, c, 10, 26))
        out.append(("fold_o", 0, c, 10, 38))
    return out


def place(fillers, steps):
    plan, left, done = {}, list(fillers), {}
    for s in steps:
        for slot in (0, 1):
            def earliest(f):
                e = f[3]
                if not isinstance(e, tuple):
                    return e
                same = [x for x in fillers if x[0] == e[1] and x[1] == f[1]]
                if not same or any((x[0], x[1], x[2]) not in done for x in same):
                    return 0 if not same else 10 ** 6
                return e[2] + max(done[x[0], x[1], x[2]] for x in same)
            can = [f for f in left if earliest(f) <= s and (f[0] not in RESIDUAL or slot == 1)]
            must = [f for f in can if f[0] in RESIDUAL]
            if not can:
                continue
            f = must[0] if must else min(can, key=lambda x: x[4])
            left.remove(f)
            plan[s, slot] = f[:3]
            done[f[:3]] = s
    assert not left, left
    for f in fillers:
        late = done[f[:3]] > f[4] + (f[0] in RESIDUAL or f[0].startswith("norm")) * 2
        assert not late, (f, done[f[:3]])
    return plan


BODY = body_fillers()
STEP_RANGE = range(CUT, CUT + STEPS)
PLAN = place(BODY, STEP_RANGE)
START = [("norm_self", 0, 0)] + [(k, 0, c) for c in range(PAIRS // 2) for k in ("q", "k")] \
    + [("v", 0, c) for c in range(2 * RT)] + [("norm_self", 1, 0)]
WARM_RANGE = range(STEPS, STEPS + CUT)
WARM = place([(k, 1, c, STEPS, STEPS + 6 + 2 * c) for c in range(PAIRS // 2) for k in ("q", "k")][:6]
             + [("v", 1, c, STEPS, STEPS + CUT - 1) for c in range(2 * RT)]
             + [(k, 1, c, STEPS, STEPS + CUT - 1) for c in (3,) for k in ("q", "k")]
             + [("norm_self", b, 0, STEPS, STEPS + CUT - 1) for b in (2, 3)], WARM_RANGE)
NEXT = {f for f in PLAN.values() if f[0] == "norm_self" or (f[0] in "qkv" and f[1] < 2)}
LAST = {k: f for k, f in PLAN.items() if f not in NEXT}
LAST_RANGE = range(CUT, max(s for s, _ in LAST) + 1)
NORMS = 3 * B


class Segment:

    def __init__(self, layer, steps, plan, fillers_before, norms_before, adds_before):
        self.layer, self.steps, self.plan = layer, steps, plan
        self.order = [plan[k] for k in sorted(plan)]
        self.fillers_before, self.norms_before, self.adds_before = fillers_before, norms_before, adds_before
        self.residual = [f for f in self.order if f[0] in RESIDUAL]
        self.normed = [f for f in self.residual if plan is not LAST or f[0] != "mlp_down"]

    def pair(self, s):
        return self.layer * STEPS + s

    def filler(self, f):
        return self.fillers_before + self.order.index(f)

    def slots(self, s):
        return [(slot, self.plan[s, slot]) for slot in (0, 1) if (s, slot) in self.plan]

    def adds(self, f):
        return self.adds_before + self.residual.index(f)

    def norm_of(self, f):
        return self.norms_before + self.normed.index(f)

    def rows_ready(self, f):
        if self.plan is WARM:
            return f[1] + 1
        source = {"norm_cross": "self_out", "norm_mlp": "cross_out", "norm_self": "mlp_down"}[f[0]]
        return self.norm_of((source, f[1], 0)) + 1

    def taken(self, used, s):
        here = [self.order.index(f) for (step, _), f in self.plan.items() if f in used and step < s]
        return self.fillers_before + max((i + 1 for i in here), default=0)


N_START = len(START) + len(WARM)
N_BODY = len(PLAN)


def warm_segment():
    return Segment(-1, WARM_RANGE, WARM, len(START), B, 0)


def body_segment(layer):
    return Segment(layer, STEP_RANGE, PLAN, layer * N_BODY + N_START, layer * NORMS + B, layer * NORMS)


def last_segment():
    layer = LAYERS - 1
    return Segment(layer, LAST_RANGE, LAST, N_START + layer * N_BODY, B + layer * NORMS, layer * NORMS)


def wait(engine, semaphore, n):
    if not isinstance(n, int) or n > 0:
        engine.wait_ge(semaphore, n)


def wait_apart(engine, semaphore, n, passed):
    engine.wait_ge(semaphore, n)
    engine.sem_inc(passed, 1)


def decoder_kernel(nc, t, out):
    ctx = ExitStack()
    with ctx:
        def sb(name, shape, dt=F32):
            return ctx.enter_context(nc.sbuf_tensor(name, shape, dt))

        def sem(name):
            return ctx.enter_context(nc.semaphore(name))

        x = sb("x", [P, B, RT, TD])
        z = sb("z", [P, B, RT, TD])
        tnT = sb("tnT", [P, B, S])
        qT = sb("qT", [P, 2, PAIRS, S])
        kT = sb("kT", [P, 2, PAIRS, S])
        v = sb("v", [P, 2, RT, H * D])
        cqT = sb("cqT", [P, 2, PAIRS, S])
        probs = sb("probs", [P, 4, RT, S])
        probsT = sb("probsT", [P, 2, RT, S])
        attT = sb("attT", [P, 2, PAIRS, S])
        neg_self = sb("neg_self", [P, B, RT, S])
        neg_cross = sb("neg_cross", [P, B, S])
        neg_none = sb("neg_none", [P, S])
        ident = sb("ident", [P, P])
        srcT = sb("srcT", [P, B, S])
        src = sb("src", [P, B, RT, SD])
        w_q = sb("w_q", [P, H * D])
        w_kv = sb("w_kv", [P, 2 * H * D])
        w_o = sb("w_o", [P, PAIRS, TD])
        cw_qT = sb("cw_qT", [P, PAIRS, TD])
        cw_kT = sb("cw_kT", [P, PAIRS, 2 * SD])
        cw_vT = sb("cw_vT", [P, PAIRS, 2 * SD])
        cw_o = sb("cw_o", [P, PAIRS, TD])
        fold_q = sb("fold_q", [P, PAIRS, 2 * SD])
        fold_o = sb("fold_o", [P, PAIRS, TD])
        w_up = sb("w_up", [P, FF])
        w_down = sb("w_down", [P, FF // P, TD])
        b_up = sb("b_up", [P, FF // P])
        upT = sb("upT", [P, FF // P, S])
        rows = sb("rows", [P, 3, TD])
        norm_gb = sb("norm_gb", [P, 2])
        pre_gb = sb("pre_gb", [P, 2])
        min_u = sb("min_u", [P, 4, RT])
        row_sum = sb("row_sum", [P, 4, RT])
        row_inv = sb("row_inv", [P, 4, RT])
        bn = sb("bn", [P, RT, 6])
        mean_var = sb("mean_var", [P, RT, 2])
        var_eps = sb("var_eps", [P, RT])
        rstd = sb("rstd", [P, RT])
        minus_half = sb("minus_half", [P, RT])
        e_wq = sb("e_wq", [P, 3, TD])
        e_wk = sb("e_wk", [SD, 3, TD])
        e_wv = sb("e_wv", [SD, 3, TD])
        e_wo = sb("e_wo", [P, 2, TD])
        e_bqkv = sb("e_bqkv", [P, 3, 3])
        e_rows = sb("e_rows", [P, 5, TD])
        e_min = sb("e_min", [P, B, RT])
        e_sum = sb("e_sum", [P, B, RT])
        e_inv = sb("e_inv", [P, B, RT])
        e_bn = sb("e_bn", [P, B, RT, 6])
        e_mv = sb("e_mv", [P, B, RT, 2])
        e_ve = sb("e_ve", [P, B, RT])
        e_rstd = sb("e_rstd", [P, B, RT])
        flat = lambda a: a[:].rearrange("p a b c -> p (a b c)")
        part = lambda a, lo, n, m: flat(a)[:, lo:lo + n * m].rearrange("p (n m) -> p n m", m=m)
        e_xT, e_qT, e_aT = (part(qT, i * B * S, B, S) for i in range(3))
        e_kT = part(kT, 0, 3 * B, S)
        e_v = part(v, 0, 3 * B * RT, TD)
        e_probs = part(cqT, 0, B * RT, S)
        e_probsT = part(cqT, B * RT * S, B * RT, S)

        scores = ctx.enter_context(nc.psum_tensor("scores", [P, 4, RT, S], F32))
        turned = ctx.enter_context(nc.psum_tensor("turned", [P, 2, RT, S], F32))
        att = ctx.enter_context(nc.psum_tensor("att", [P, 512], F32))
        proj = ctx.enter_context(nc.psum_tensor("proj", [P, 512], F32))
        e_a = [turned[:, 0], turned[:, 1], att[:, :].rearrange("p (a b) -> p a b", a=RT),
               proj[:, :].rearrange("p (a b) -> p a b", a=RT)]
        e_b = [scores[:, i] for i in range(4)]

        x_loaded, consts_loaded, masks_loaded = sem("x_loaded"), sem("consts_loaded"), sem("masks_loaded")
        ctx_loaded, e_loaded = sem("ctx_loaded"), sem("e_loaded")
        qkv_loaded, attw_loaded, mlp_loaded = sem("qkv_loaded"), sem("attw_loaded"), sem("mlp_loaded")
        ident_zeroed, ident_ready = sem("ident_zeroed"), sem("ident_ready")
        blocks_zeroed, neg_ready = sem("blocks_zeroed"), sem("neg_ready")
        half_ready = sem("half_ready")
        scores_ready, turned_ready, att_ready, proj_ready = (
            sem("scores_ready"), sem("turned_ready"), sem("att_ready"), sem("proj_ready"))
        proj_taken = sem("proj_taken")
        shifted = sem("shifted")
        exp_done, inv_ready, probs_ready = sem("exp_done"), sem("inv_ready"), sem("probs_ready")
        turned_taken, att_taken = sem("turned_taken"), sem("att_taken")
        bn_ready, mv_ready, var_ready, rstd_ready, z_ready = (
            sem("bn_ready"), sem("mv_ready"), sem("var_ready"), sem("rstd_ready"), sem("z_ready"))
        bias_added = sem("bias_added")
        waits_passed = sem("waits_passed")
        E = {n: sem("e_" + n) for n in (
            "ctx_proj", "ctx_taken", "biased", "xT_ps", "xT", "q_ps", "q", "s_ps", "shifted", "exp", "inv", "norm",
            "pT_ps", "pT", "a_ps", "a", "o_ps", "x", "bn", "mv", "var", "rstd", "z", "zg")}
        stored = sem("stored")

        QKV_DMAS, ATTW_DMAS, MLP_DMAS = 2, 8, 7

        def load_qkv(q, l):
            q.dma_start(w_q[:, :], t["sa_q"][l]).then_inc(qkv_loaded, 16)
            q.dma_start(w_kv[:, :], t["sa_kv"][l]).then_inc(qkv_loaded, 16)

        def load_attw(q, l):
            pairs = "(c r) m -> r c m"
            q.dma_start(w_o[:, :, :], t["sa_ow"][l].rearrange(pairs, r=P)).then_inc(attw_loaded, 16)
            q.dma_start(rows[:, 0, :], t["sa_ob"][l:l + 1, :].partition_broadcast(P)
                        if isinstance(l, int) else t["sa_ob"][bass.ds(l, 1), :].partition_broadcast(P)
                        ).then_inc(attw_loaded, 16)
            q.dma_start(cw_qT[:, :, :], t["ca_qT"][l].rearrange(pairs, r=P)).then_inc(attw_loaded, 16)
            q.dma_start(cw_o[:, :, :], t["ca_ow"][l].rearrange(pairs, r=P)).then_inc(attw_loaded, 16)
            for j in range(2):
                at = slice(j * D, (j + 1) * D)
                for w, first in ((cw_kT, 0), (cw_vT, H * D)):
                    blocks = t["ca_kvT"][l][first:first + H * D].rearrange("(c h r) m -> h r c m", h=2, r=D)
                    q.dma_start(w[at, :, j * SD:(j + 1) * SD], blocks[j]).then_inc(attw_loaded, 16)

        def load_mlp(q, l):
            row = (lambda n: t[n][l:l + 1, :]) if isinstance(l, int) else (lambda n: t[n][bass.ds(l, 1), :])
            q.dma_start(w_up[:, :], t["ff_w1"][l]).then_inc(mlp_loaded, 16)
            q.dma_start(w_down[:, :, :], t["ff_w2"][l].rearrange("(c r) m -> r c m", r=P)).then_inc(mlp_loaded, 16)
            q.dma_start(b_up[:, :], row("ff_b1").rearrange("a (c r) -> r (a c)", r=P)).then_inc(mlp_loaded, 16)
            q.dma_start(rows[:, 1, :], row("ca_ob").partition_broadcast(P)).then_inc(mlp_loaded, 16)
            q.dma_start(rows[:, 2, :], row("ff_b2").partition_broadcast(P)).then_inc(mlp_loaded, 16)
            q.dma_start(pre_gb[:, 0:1], row("pre_g").rearrange("a r -> r a")).then_inc(mlp_loaded, 16)
            q.dma_start(pre_gb[:, 1:2], row("pre_b").rearrange("a r -> r a")).then_inc(mlp_loaded, 16)

        ctx.enter_context(nc.allow_non_contiguous_dma("biases and gains onto partitions"))
        block = ctx.enter_context(nc.Block())

        @block.sync
        def _(sp):
            sp.dma_start(x[:, :, :, :], t["x"].rearrange("b (r p) d -> p b r d", p=P)).then_inc(x_loaded, 16)
            col = lambda n: t[n].rearrange("(r a) -> r a", a=1)
            sp.dma_start(norm_gb[:, 0:1], col("norm_g")).then_inc(consts_loaded, 16)
            sp.dma_start(norm_gb[:, 1:2], col("norm_b")).then_inc(consts_loaded, 16)
            load_qkv(sp, 0)
            sp.dma_start(neg_self[:, :, :, :].bitcast(I32),
                         t["mask_self"].rearrange("b (r p) k -> p b r k", p=P)).then_inc(masks_loaded, 16)
            sp.dma_start(neg_cross[:, :, :].bitcast(I32).rearrange("p b k -> p (b k)"),
                         t["mask_cross"].rearrange("b a k -> a (b k)").partition_broadcast(P)).then_inc(masks_loaded, 16)
            for j in range(2):
                sp.dma_start(srcT[j * SD:(j + 1) * SD, :, :], t["srcT"][:, :, :]).then_inc(ctx_loaded, 16)
            sp.dma_start(src[:, :, :, :], t["ctx"].rearrange("b (r p) d -> p b r d", p=P)).then_inc(ctx_loaded, 16)
            sp.wait_ge(blocks_zeroed, 2)
            load_attw(sp, 0)
            load_mlp(sp, 0)
            for n, name in enumerate(("L1", "L2", "L3")):
                sp.dma_start(e_wq[:, n, :], t[name + "_Wq"]).then_inc(e_loaded, 16)
                sp.dma_start(e_wk[:, n, :], t[name + "_Wk"]).then_inc(e_loaded, 16)
                sp.dma_start(e_wv[:, n, :], t[name + "_Wv"]).then_inc(e_loaded, 16)
                for i, bias in enumerate(("_bq", "_bk", "_bv")):
                    sp.dma_start(e_bqkv[:, n, i:i + 1], col(name + bias)).then_inc(e_loaded, 16)
            sp.dma_start(e_wo[:, 0, :], t["L1_Wo"]).then_inc(e_loaded, 16)
            sp.dma_start(e_wo[:, 1, :], t["L3_Wo"]).then_inc(e_loaded, 16)
            for i, name in enumerate(("L1_bo", "L3_bo", "L2_bv", "L2_gamma", "L2_beta")):
                sp.dma_start(e_rows[:, i, :], t[name].rearrange("(a n) -> a n", a=1).partition_broadcast(P)
                             ).then_inc(e_loaded, 16)
            with sp.Fori(0, LAYERS - 1) as l:
                seg = body_segment(l)
                wait_apart(sp, scores_ready, seg.pair(26), waits_passed)
                load_qkv(sp, l + 1)
                wait_apart(sp, scores_ready, seg.pair(41), waits_passed)
                wait_apart(sp, bias_added, seg.adds_before + B, waits_passed)
                load_attw(sp, l + 1)
                wait_apart(sp, scores_ready, seg.pair(72), waits_passed)
                wait_apart(sp, bias_added, seg.adds_before + NORMS, waits_passed)
                load_mlp(sp, l + 1)
            for b in range(B):
                sp.wait_ge(E["x"], 2 * B + b + 1)
                sp.dma_start(out[b].rearrange("(r p) d -> p r d", p=P), x[:, b]).then_inc(stored, 16)
            sp.wait_ge(stored, 16 * B)

        E_DMAS = 3 * 6 + 2 + 5

        @block.tensor
        def _(pe):
            def pair_scores(seg, s):
                layer_s = s % STEPS
                cross, b, c = layer_s >= SELF, layer_s % SELF // PAIRS, layer_s % PAIRS
                for r in range(RT):
                    for j in range(2):
                        at = slice(j * D, (j + 1) * D)
                        q, k = (cqT, srcT[at, b, :]) if cross else (qT, kT[at, b % 2, c, :])
                        mm = nc.tensor.matmul(scores[:, 2 * (s % 2) + j, r, :], q[at, b % 2, c, r * P:(r + 1) * P],
                                              k, start=True, stop=True)
                mm.then_inc(scores_ready, 1)

            def pair_turn(seg, s, j):
                pe.wait_ge(probs_ready, seg.pair(s) * 2 + j + 1)
                wait(pe, turned_taken, (seg.pair(s) - 1) * 2 + j + 1)
                for k in range(RT):
                    for r in range(RT):
                        mm = nc.tensor.transpose(turned[:, j, k, r * P:(r + 1) * P],
                                                 probs[:, 2 * (s % 2) + j, r, k * P:(k + 1) * P], ident[:, :])
                mm.then_inc(turned_ready, 1)

            def pair_values(seg, s):
                layer_s = s % STEPS
                cross, b, c = layer_s >= SELF, layer_s % SELF // PAIRS, layer_s % PAIRS
                pe.wait_ge(turned_taken, (seg.pair(s) + 1) * 2)
                wait(pe, att_taken, seg.pair(s))
                if not cross and c == 0:
                    pe.wait_ge(proj_taken, seg.taken([("v", b, i) for i in range(2 * RT)], s))
                for k in range(RT):
                    for j in range(2):
                        val = src[:, b, k, :] if cross else v[:, b % 2, k, (2 * c + j) * D:(2 * c + j + 1) * D]
                        mm = nc.tensor.matmul(att[j * D:(j + 1) * D, 0:S], val, probsT[:, j, k, :],
                                              start=(k == 0), stop=(k == RT - 1))
                mm.then_inc(att_ready, 1)

            def filler(seg, f, weights):
                kind, b, c = f
                n = seg if isinstance(seg, int) else seg.filler(f)
                wait(pe, proj_taken, n)
                if kind in ("norm_self", "norm_cross", "norm_mlp"):
                    pe.wait_ge(z_ready, weights)
                    for r in range(RT):
                        mm = nc.tensor.transpose(proj[:, r * P:(r + 1) * P], z[:, b, r, :], ident[:, :])
                elif kind in ("q", "k", "cq"):
                    if weights is not None:
                        pe.wait_ge(qkv_loaded, weights)
                    w = {"q": w_q[:, :], "k": w_kv[:, :], "cq": fold_q[:, :, :].rearrange("p c m -> p (c m)")}[kind]
                    for i in range(2):
                        mm = nc.tensor.matmul(proj[:, i * S:(i + 1) * S], w[:, (2 * c + i) * P:(2 * c + i + 1) * P],
                                              tnT[:, b, :], start=True, stop=True)
                elif kind == "v":
                    half, r = c // RT, c % RT
                    first = H * D + half * 512
                    mm = nc.tensor.matmul(proj[:, :], tnT[:, b, r * P:(r + 1) * P], w_kv[:, first:first + 512],
                                          start=True, stop=True)
                elif kind == "fold_q":
                    pe.wait_ge(attw_loaded, weights)
                    for i in range(4):
                        mm = nc.tensor.matmul(proj[:, i * P:(i + 1) * P], cw_qT[:, 4 * c + i, :],
                                              cw_kT[:, 4 * c + i, :], start=True, stop=True)
                elif kind == "fold_o":
                    pe.wait_ge(attw_loaded, weights)
                    for i in range(4):
                        mm = nc.tensor.matmul(proj[:, i * P:(i + 1) * P], cw_vT[:, 4 * c + i, :],
                                              cw_o[:, 4 * c + i, :], start=True, stop=True)
                elif kind in ("self_out", "cross_out"):
                    pe.wait_ge(att_taken, weights[0])
                    pe.wait_ge(attw_loaded, weights[1])
                    w = w_o if kind == "self_out" else fold_o
                    for r in range(RT):
                        for i in range(PAIRS):
                            mm = nc.tensor.matmul(proj[:, r * P:(r + 1) * P], attT[:, b % 2, i, r * P:(r + 1) * P],
                                                  w[:, i, :], start=(i == 0), stop=(i == PAIRS - 1))
                elif kind == "mlp_up":
                    pe.wait_ge(mlp_loaded, weights)
                    for i in range(2):
                        mm = nc.tensor.matmul(proj[:, i * S:(i + 1) * S], w_up[:, (2 * c + i) * P:(2 * c + i + 1) * P],
                                              tnT[:, b, :], start=True, stop=True)
                elif kind == "mlp_down":
                    for r in range(RT):
                        for i in range(FF // P):
                            mm = nc.tensor.matmul(proj[:, r * P:(r + 1) * P], upT[:, i, r * P:(r + 1) * P],
                                                  w_down[:, i, :], start=(i == 0), stop=(i == FF // P - 1))
                mm.then_inc(proj_ready, 1)

            def weights_of(seg, s, f):
                kind, b, c = f
                if kind.startswith("norm"):
                    return seg.rows_ready(f)
                if kind in "qkv":
                    return 16 * QKV_DMAS * (seg.layer + 2) if b == 0 else None
                if kind == "self_out":
                    return seg.pair(PAIRS * (b + 1)), 16 * ATTW_DMAS * (seg.layer + 1)
                if kind == "cross_out":
                    return seg.pair(SELF + PAIRS * (b + 1)), 16 * ATTW_DMAS * (seg.layer + 1)
                if kind.startswith("fold"):
                    return 16 * ATTW_DMAS * (seg.layer + 1)
                if kind == "mlp_up":
                    return 16 * MLP_DMAS * (seg.layer + 1)
                return None

            def steps(seg, final=False):
                for s in seg.steps:
                    slots = dict(seg.slots(s))
                    if not (final and s >= STEPS - 1):
                        c, b = (s + 1) % PAIRS, (s + 1) % SELF // PAIRS
                        kinds = ("cq",) if (s + 1) % STEPS >= SELF else ("q", "k")
                        if c % 2 == 0:
                            pe.wait_ge(proj_taken, seg.taken([(kind, b, c // 2) for kind in kinds], s + 1))
                        pair_scores(seg, s + 1)
                    if 0 in slots:
                        filler(seg, slots[0], weights_of(seg, s, slots[0]))
                    if not (final and s >= STEPS):
                        pair_turn(seg, s, 0)
                        pair_turn(seg, s, 1)
                    if 1 in slots:
                        filler(seg, slots[1], weights_of(seg, s, slots[1]))
                    if not (final and s >= STEPS):
                        pair_values(seg, s)

            pe.wait_ge(ident_ready, 1)
            pe.wait_ge(qkv_loaded, 16 * QKV_DMAS)
            for n, f in enumerate(START):
                filler(n, f, {0: 1, 1: 2}[f[1]] if f[0] == "norm_self" else None)
            pe.wait_ge(proj_taken, len(START))
            first = warm_segment()
            pair_scores(first, STEPS)
            steps(first)
            pe.wait_ge(ctx_loaded, 16 * 3)
            with pe.Fori(0, LAYERS - 1) as l:
                steps(body_segment(l))
            steps(last_segment(), final=True)

            pe.wait_ge(e_loaded, 16 * E_DMAS)
            n = 0
            for net in range(3):
                for b in range(B):
                    if n >= 4:
                        pe.wait_ge(E["ctx_taken"], n - 3)
                    if n == 0:
                        pe.wait_ge(proj_taken, N_START + (LAYERS - 1) * N_BODY + len(LAST))
                        pe.wait_ge(att_taken, LAYERS * STEPS)
                    nc.tensor.matmul(scores[:, n % 4, 0, :], e_wk[:, net, :], srcT[0:SD, b, :], start=True, stop=True)
                    for r in range(RT):
                        mm = nc.tensor.matmul(scores[:, n % 4, 1, r * P:(r + 1) * P],
                                              srcT[0:SD, b, r * P:(r + 1) * P], e_wv[:, net, :], start=True, stop=True)
                    mm.then_inc(E["ctx_proj"], 1)
                    n += 1
            for net in range(3):
                for b in range(B):
                    if net:
                        pe.wait_ge(E["x"], (net - 1) * B + b + 1)
                    for r in range(RT):
                        mm = nc.tensor.transpose(e_a[b][:, 0, r * P:(r + 1) * P], x[:, b, r, :], ident[:, :])
                    mm.then_inc(E["xT_ps"], 1)
                for b in range(B):
                    pe.wait_ge(E["xT"], net * B + b + 1)
                    nc.tensor.matmul(e_a[b][:, 0, :], e_wq[:, net, :], e_xT[:, b, :], start=True, stop=True
                                     ).then_inc(E["q_ps"], 1)
                if net == 0:
                    pe.wait_ge(E["ctx_taken"], 3 * B)
                for b in range(B):
                    pe.wait_ge(E["q"], net * B + b + 1)
                    for r in range(RT):
                        at = slice(r * P, (r + 1) * P)
                        lhs, rhs = (e_kT[:, B + b, at], e_qT[:, b, :]) if net == 1 else (
                            e_qT[:, b, at], e_kT[:, net * B + b, :])
                        mm = nc.tensor.matmul(e_b[b][:, r, :], lhs, rhs, start=True, stop=True)
                    mm.then_inc(E["s_ps"], 1)
                if net == 1:
                    for b in range(B):
                        pe.wait_ge(E["norm"], B + b + 1)
                        for r in range(RT):
                            for k in range(RT):
                                mm = nc.tensor.matmul(e_a[b][:, 0, r * P:(r + 1) * P],
                                                      e_probs[:, b * RT + k, r * P:(r + 1) * P],
                                                      e_v[:, (B + b) * RT + k, :], start=(k == 0), stop=(k == RT - 1))
                        mm.then_inc(E["o_ps"], 1)
                    continue
                m = 0 if net == 0 else 1
                for b in range(B):
                    pe.wait_ge(E["norm"], net * B + b + 1)
                    for k in range(RT):
                        for r in range(RT):
                            mm = nc.tensor.transpose(e_a[b][:, k, r * P:(r + 1) * P],
                                                     e_probs[:, b * RT + r, k * P:(k + 1) * P], ident[:, :])
                    mm.then_inc(E["pT_ps"], 1)
                for b in range(B):
                    pe.wait_ge(E["pT"], m * B + b + 1)
                    for k in range(RT):
                        mm = nc.tensor.matmul(e_b[b][:, 0, :], e_v[:, (net * B + b) * RT + k, :],
                                              e_probsT[:, b * RT + k, :], start=(k == 0), stop=(k == RT - 1))
                    mm.then_inc(E["a_ps"], 1)
                for b in range(B):
                    pe.wait_ge(E["a"], m * B + b + 1)
                    for r in range(RT):
                        mm = nc.tensor.matmul(e_a[b][:, 0, r * P:(r + 1) * P], e_aT[:, b, r * P:(r + 1) * P],
                                              e_wo[:, m, :], start=True, stop=True)
                    mm.then_inc(E["o_ps"], 1)

        @block.scalar
        def _(act):
            def exps(seg, s, j):
                act.wait_ge(shifted, seg.pair(s) * 2 + j + 1)
                slot = 2 * (s % 2) + j
                for r in range(RT):
                    e = nc.scalar.activation(probs[:, slot, r, :], scores[:, slot, r, :], ACT.Exp,
                                             bias=min_u[:, slot, r:r + 1], scale=-1.0,
                                             accum_out=row_sum[:, slot, r:r + 1])
                e.then_inc(exp_done, 1)

            def take_att(seg, s):
                layer_s = s % STEPS
                b, c = layer_s % SELF // PAIRS, layer_s % PAIRS
                act.wait_ge(att_ready, seg.pair(s) + 1)
                nc.scalar.activation(attT[:, b % 2, c, :], att[:, 0:S], ACT.Copy).then_inc(att_taken, 1)

            def take(n, f, layer):
                kind, b, c = f
                act.wait_ge(proj_ready, n + 1)
                halves = proj[:, :].rearrange("p (a b) -> p a b", a=2)
                quarters = proj[:, :].rearrange("p (a b) -> p a b", a=4)
                if kind.startswith("norm"):
                    if kind == "norm_mlp":
                        act.wait_ge(mlp_loaded, 16 * MLP_DMAS * (layer + 1))
                    gb = pre_gb if kind == "norm_mlp" else norm_gb
                    nc.scalar.activation(tnT[:, b, :], proj[:, 0:S], ACT.Identity, scale=gb[:, 0:1], bias=gb[:, 1:2]
                                         ).then_inc(proj_taken, 1)
                elif kind == "mlp_up":
                    for i in range(2):
                        a = nc.scalar.activation(upT[:, 2 * c + i, :], proj[:, i * S:(i + 1) * S], ACT.Relu,
                                                 bias=b_up[:, 2 * c + i:2 * c + i + 1])
                    a.then_inc(proj_taken, 1)
                else:
                    dst, src_ap = {
                        "q": lambda: (qT[:, b % 2, 2 * c:2 * c + 2, :], halves),
                        "k": lambda: (kT[:, b % 2, 2 * c:2 * c + 2, :], halves),
                        "cq": lambda: (cqT[:, b % 2, 2 * c:2 * c + 2, :], halves),
                        "v": lambda: (v[:, b % 2, c % RT, (c // RT) * 512:(c // RT + 1) * 512], proj[:, :]),
                        "fold_q": lambda: (fold_q[:, 4 * c:4 * c + 4, :], quarters),
                        "fold_o": lambda: (fold_o[:, 4 * c:4 * c + 4, :], quarters),
                    }[kind]()
                    nc.scalar.activation(dst, src_ap, ACT.Copy).then_inc(proj_taken, 1)

            def steps(seg, final=False):
                for s in seg.steps:
                    slots = {k: f for k, f in seg.slots(s) if f[0] not in RESIDUAL}
                    if s > seg.steps[0] and not (final and s > STEPS):
                        take_att(seg, s - 1)
                    heads = not (final and s >= STEPS - 1)
                    if heads:
                        exps(seg, s + 1, 0)
                    if 0 in slots:
                        take(seg.filler(slots[0]), slots[0], seg.layer)
                    if heads:
                        exps(seg, s + 1, 1)
                    if 1 in slots:
                        take(seg.filler(slots[1]), slots[1], seg.layer)
                if not final:
                    take_att(seg, seg.steps[-1])

            act.wait_ge(consts_loaded, 32)
            for n, f in enumerate(START):
                take(n, f, 0)
            seg = warm_segment()
            exps(seg, STEPS, 0)
            exps(seg, STEPS, 1)
            steps(seg)
            with act.Fori(0, LAYERS - 1) as l:
                steps(body_segment(l))
            steps(last_segment(), final=True)

            act.wait_ge(e_loaded, 16 * E_DMAS)
            for n in range(3 * B):
                net, b = n // B, n % B
                act.wait_ge(E["ctx_proj"], n + 1)
                nc.scalar.activation(e_kT[:, n, :], scores[:, n % 4, 0, :], ACT.Identity, bias=e_bqkv[:, net, 1:2])
                nc.scalar.activation(e_v[:, n * RT:(n + 1) * RT, :],
                                     scores[:, n % 4, 1, :].rearrange("p (a b) -> p a b", a=RT), ACT.Copy
                                     ).then_inc(E["ctx_taken"], 1)
            for net in range(3):
                for b in range(B):
                    act.wait_ge(E["xT_ps"], net * B + b + 1)
                    nc.scalar.activation(e_xT[:, b, :], e_a[b][:, 0, :], ACT.Copy).then_inc(E["xT"], 1)
                for b in range(B):
                    act.wait_ge(E["q_ps"], net * B + b + 1)
                    nc.scalar.activation(e_qT[:, b, :], e_a[b][:, 0, :], ACT.Identity, bias=e_bqkv[:, net, 0:1]
                                         ).then_inc(E["q"], 1)
                for b in range(B):
                    act.wait_ge(E["shifted"], net * B + b + 1)
                    for r in range(RT):
                        e = nc.scalar.activation(e_probs[:, b * RT + r, :], e_b[b][:, r, :], ACT.Exp,
                                                 bias=e_min[:, b, r:r + 1], scale=-1.0, accum_out=e_sum[:, b, r:r + 1])
                    e.then_inc(E["exp"], 1)
                if net == 1:
                    continue
                m = 0 if net == 0 else 1
                for b in range(B):
                    act.wait_ge(E["pT_ps"], m * B + b + 1)
                    nc.scalar.activation(e_probsT[:, b * RT:(b + 1) * RT, :], e_a[b], ACT.Copy).then_inc(E["pT"], 1)
                for b in range(B):
                    act.wait_ge(E["a_ps"], m * B + b + 1)
                    nc.scalar.activation(e_aT[:, b, :], e_b[b][:, 0, :], ACT.Identity, bias=e_bqkv[:, net, 2:3]
                                         ).then_inc(E["a"], 1)

        @block.vector
        def _(dve):
            def shift(seg, s, j):
                layer_s = s % STEPS
                cross, b = layer_s >= SELF, layer_s % SELF // PAIRS
                slot = 2 * (s % 2) + j
                if j == 0:
                    dve.wait_ge(neg_ready, 3)
                    wait_apart(dve, scores_ready, seg.pair(s) + 1, waits_passed)
                for r in range(RT):
                    d = nc.vector.tensor_tensor_reduce(
                        out=scores[:, slot, r, :], in0=scores[:, slot, r, :],
                        in1=neg_cross[:, b, :] if cross else neg_self[:, b, r, :], scale=-SCALE, scalar=3e38,
                        op0=ALU.add, op1=ALU.min, accum_out=min_u[:, slot, r:r + 1])
                d.then_inc(shifted, 1)

            def invert(seg, s, j):
                slot = 2 * (s % 2) + j
                dve.wait_ge(exp_done, seg.pair(s) * 2 + j + 1)
                nc.vector.reciprocal(row_inv[:, slot, :], row_sum[:, slot, :]).then_inc(inv_ready, 1)

            def take_turned(seg, s, j):
                dve.wait_ge(turned_ready, seg.pair(s) * 2 + j + 1)
                nc.vector.tensor_copy(probsT[:, j, :, :], turned[:, j, :, :]).then_inc(turned_taken, 1)

            def stats(b, n):
                for r in range(RT):
                    d = nc.vector.bn_stats(bn[:, r, :], x[:, b, r, :])
                d.then_inc(bn_ready, 1)
                wait_apart(dve, bn_ready, n + 1, waits_passed)
                for r in range(RT):
                    d = nc.vector.bn_aggr(mean_var[:, r, :], bn[:, r, :])
                d.then_inc(mv_ready, 1)
                dve.wait_ge(mv_ready, n + 1)
                nc.vector.tensor_scalar(var_eps[:, :], mean_var[:, :, 1], EPS, None, ALU.add).then_inc(var_ready, 1)

            def normalise(b, n):
                dve.wait_ge(rstd_ready, n + 1)
                for r in range(RT):
                    d = nc.vector.tensor_scalar(z[:, b, r, :], x[:, b, r, :], mean_var[:, r, 0:1], rstd[:, r:r + 1],
                                                ALU.subtract, ALU.mult)
                d.then_inc(z_ready, 1)

            def add(seg, f):
                dve.wait_ge(proj_ready, seg.filler(f) + 1)
                dve.wait_ge(bias_added, seg.adds(f) + 1)
                nc.vector.tensor_tensor(x[:, f[1]], proj[:, 0:S].rearrange("p (a b) -> p a b", a=RT), x[:, f[1]],
                                        ALU.add).then_inc(proj_taken, 1)

            def steps(seg, final=False):
                waiting = []
                for s in seg.steps:
                    heads = not (final and s >= STEPS - 1)
                    turns = not (final and s >= STEPS)
                    if heads:
                        shift(seg, s + 1, 0)
                        shift(seg, s + 1, 1)
                    if turns:
                        take_turned(seg, s, 0)
                    if heads:
                        invert(seg, s + 1, 0)
                    if turns:
                        take_turned(seg, s, 1)
                    if heads:
                        invert(seg, s + 1, 1)
                    for f in waiting:
                        normalise(f[1], seg.norm_of(f))
                    waiting = [f for _, f in seg.slots(s) if f[0] in RESIDUAL]
                    for f in waiting:
                        add(seg, f)
                        if f in seg.normed:
                            dve.wait_ge(proj_taken, seg.filler(f) + 1)
                            stats(f[1], seg.norm_of(f))
                    waiting = [f for f in waiting if f in seg.normed]
                assert not waiting

            nc.vector.memset(minus_half[:, :], -0.5).then_inc(half_ready, 1)
            nc.vector.memset(cw_kT[:, :, :], 0.0).then_inc(blocks_zeroed, 1)
            nc.vector.memset(cw_vT[:, :, :], 0.0).then_inc(blocks_zeroed, 1)
            dve.wait_ge(x_loaded, 16)
            for b in range(B):
                stats(b, b)
                normalise(b, b)
            dve.wait_ge(masks_loaded, 32)
            for m in (neg_self[:, :, :, :].rearrange("p a b c -> p (a b c)"), neg_cross[:, :, :].rearrange("p a b -> p (a b)")):
                nc.vector.tensor_scalar(m, m.bitcast(I32), 0, MASKED, ALU.is_equal, ALU.mult).then_inc(neg_ready, 1)
            nc.vector.memset(neg_none[:, :], 0.0).then_inc(neg_ready, 1)
            dve.wait_ge(neg_ready, 3)
            seg = warm_segment()
            shift(seg, STEPS, 0)
            shift(seg, STEPS, 1)
            invert(seg, STEPS, 0)
            invert(seg, STEPS, 1)
            steps(seg)
            with dve.Fori(0, LAYERS - 1) as l:
                steps(body_segment(l))
            steps(last_segment(), final=True)

            dve.wait_ge(e_loaded, 16 * E_DMAS)
            for n in range(B, 2 * B):
                dve.wait_ge(E["ctx_taken"], n + 1)
                for r in range(RT):
                    nc.vector.tensor_tensor(e_v[:, n * RT + r, :], e_v[:, n * RT + r, :], e_rows[:, 2, :], ALU.add)
            for net in range(3):
                for b in range(B):
                    dve.wait_ge(E["s_ps"], net * B + b + 1)
                    for r in range(RT):
                        d = nc.vector.tensor_tensor_reduce(
                            out=e_b[b][:, r, :], in0=e_b[b][:, r, :], in1=neg_none[:, :], scale=-SCALE1, scalar=3e38,
                            op0=ALU.add, op1=ALU.min, accum_out=e_min[:, b, r:r + 1])
                    d.then_inc(E["shifted"], 1)
                for b in range(B):
                    dve.wait_ge(E["exp"], net * B + b + 1)
                    nc.vector.reciprocal(e_inv[:, b, :], e_sum[:, b, :]).then_inc(E["inv"], 1)
                for b in range(B):
                    dve.wait_ge(E["inv"], net * B + b + 1)
                    for r in range(RT):
                        d = nc.vector.tensor_scalar(e_probs[:, b * RT + r, :], e_probs[:, b * RT + r, :],
                                                    e_inv[:, b, r:r + 1], None, ALU.mult)
                    d.then_inc(E["norm"], 1)
                for b in range(B):
                    dve.wait_ge(E["o_ps"], net * B + b + 1)
                    if net != 1:
                        dve.wait_ge(E["biased"], (B if net == 2 else 0) + b + 1)
                    d = nc.vector.tensor_tensor(x[:, b], e_a[b][:, 0, :].rearrange("p (a b) -> p a b", a=RT), x[:, b],
                                                ALU.add)
                    d.then_inc(E["z"] if net == 1 else E["x"], 1)
                if net != 1:
                    continue
                for b in range(B):
                    dve.wait_ge(E["z"], b + 1)
                    for r in range(RT):
                        d = nc.vector.bn_stats(e_bn[:, b, r, :], x[:, b, r, :])
                    d.then_inc(E["bn"], 1)
                for b in range(B):
                    dve.wait_ge(E["bn"], b + 1)
                    for r in range(RT):
                        d = nc.vector.bn_aggr(e_mv[:, b, r, :], e_bn[:, b, r, :])
                    d.then_inc(E["mv"], 1)
                for b in range(B):
                    dve.wait_ge(E["mv"], b + 1)
                    nc.vector.tensor_scalar(e_ve[:, b, :], e_mv[:, b, :, 1], EPS2, None, ALU.add).then_inc(E["var"], 1)
                for b in range(B):
                    dve.wait_ge(E["rstd"], b + 1)
                    for r in range(RT):
                        d = nc.vector.tensor_scalar(x[:, b, r, :], x[:, b, r, :], e_mv[:, b, r, 0:1],
                                                    e_rstd[:, b, r:r + 1], ALU.subtract, ALU.mult)
                    d.then_inc(E["z"], 1)
                for b in range(B):
                    dve.wait_ge(E["z"], B + b + 1)
                    for r in range(RT):
                        d = nc.vector.tensor_tensor(x[:, b, r, :], x[:, b, r, :], e_rows[:, 3, :], ALU.mult)
                    d.then_inc(E["zg"], 1)
                for b in range(B):
                    dve.wait_ge(E["zg"], b + 1)
                    for r in range(RT):
                        d = nc.vector.tensor_tensor(x[:, b, r, :], x[:, b, r, :], e_rows[:, 4, :], ALU.add)
                    d.then_inc(E["x"], 1)

        @block.gpsimd
        def _(pool):
            def scale_probs(seg, s, j):
                slot = 2 * (s % 2) + j
                wait_apart(pool, inv_ready, seg.pair(s) * 2 + j + 1, waits_passed)
                for r in range(RT):
                    g = nc.gpsimd.tensor_scalar(probs[:, slot, r, :], probs[:, slot, r, :], row_inv[:, slot, r:r + 1],
                                                1.0, ALU.mult, ALU.mult)
                g.then_inc(probs_ready, 1)

            def root(n):
                pool.wait_ge(var_ready, n + 1)
                nc.gpsimd.tensor_tensor(rstd[:, :], var_eps[:, :], minus_half[:, :], ALU.pow).then_inc(rstd_ready, 1)

            def add_bias(seg, f):
                kind, b, _ = f
                i = RESIDUAL.index(kind)
                if i == 0:
                    pool.wait_ge(attw_loaded, 16 * ATTW_DMAS * (seg.layer + 1))
                    pool.wait_ge(z_ready, seg.norms_before)
                else:
                    pool.wait_ge(mlp_loaded, 16 * MLP_DMAS * (seg.layer + 1))
                    pool.wait_ge(z_ready, seg.norm_of((RESIDUAL[i - 1], b, 0)) + 1)
                for r in range(RT):
                    g = nc.gpsimd.tensor_tensor(x[:, b, r, :], x[:, b, r, :], rows[:, i, :], ALU.add)
                g.then_inc(bias_added, 1)

            def steps(seg, final=False):
                for s in seg.steps:
                    residual = [f for _, f in seg.slots(s) if f[0] in RESIDUAL]
                    for f in residual:
                        add_bias(seg, f)
                    if not (final and s >= STEPS - 1):
                        scale_probs(seg, s + 1, 0)
                        scale_probs(seg, s + 1, 1)
                    for f in residual:
                        if f in seg.normed:
                            root(seg.norm_of(f))

            nc.gpsimd.memset(ident[:, :], 0.0).then_inc(ident_zeroed, 1)
            pool.wait_ge(ident_zeroed, 1)
            nc.gpsimd.affine_select(out=ident[:, :], in_=ident[:, :], compare_op=ALU.not_equal, fill=1.0, base=0,
                                    pattern=[[-1, P]], channel_multiplier=1).then_inc(ident_ready, 1)
            pool.wait_ge(half_ready, 1)
            for b in range(B):
                root(b)
            seg = warm_segment()
            scale_probs(seg, STEPS, 0)
            scale_probs(seg, STEPS, 1)
            steps(seg)
            with pool.Fori(0, LAYERS - 1) as l:
                steps(body_segment(l))
            steps(last_segment(), final=True)

            pool.wait_ge(e_loaded, 16 * E_DMAS)
            for m, net in enumerate((0, 2)):
                if net == 2:
                    for b in range(B):
                        pool.wait_ge(E["var"], b + 1)
                        nc.gpsimd.tensor_tensor(e_rstd[:, b, :], e_ve[:, b, :], minus_half[:, :], ALU.pow
                                                ).then_inc(E["rstd"], 1)
                for b in range(B):
                    pool.wait_ge(E["xT_ps"], net * B + b + 1)
                    for r in range(RT):
                        g = nc.gpsimd.tensor_tensor(x[:, b, r, :], x[:, b, r, :], e_rows[:, m, :], ALU.add)
                    g.then_inc(E["biased"], 1)


def kernel(**inputs):
    import numpy as np
    import concourse.bacc as bacc
    from concourse.bass_utils import run_bass_kernel_spmd

    a = {k: np.asarray(v) for k, v in inputs.items()}
    data = {"x": a["x"], "ctx": a["ctx_512"], "srcT": a["ctx_512"].transpose(2, 0, 1),
            "mask_self": a["mask_BxSxS_ik0"], "mask_cross": a["mask_Bx1xS2_if1"],
            "ca_qT": a["L0_xattn_ca_q"].transpose(0, 2, 1), "ca_kvT": a["L0_xattn_ca_kv"].transpose(0, 2, 1)}
    for n in ("norm_g", "norm_b", "sa_kv", "sa_q", "sa_ow", "sa_ob", "ca_ow", "ca_ob", "ff_w1", "ff_b1", "ff_w2",
              "ff_b2", "pre_g", "pre_b"):
        data[n] = a["L0_xattn_" + n]
    for net, names in (("L1", ("Wq", "bq", "Wk", "bk", "Wv", "bv", "Wo", "bo")),
                       ("L2", ("Wq", "bq", "Wk", "bk", "Wv", "bv", "gamma", "beta")),
                       ("L3", ("Wq", "bq", "Wk", "bk", "Wv", "bv", "Wo", "bo"))):
        for n in names:
            data[net + "_" + n] = a[net + "_xattn_" + n]
    nc = bacc.Bacc("TRN2", target_bir_lowering=False, num_devices=1)
    arrays, t = {}, {}
    for n, arr in data.items():
        arr = np.ascontiguousarray(arr)
        arrays["in_" + n] = arr
        t[n] = nc.dram_tensor("in_" + n, arr.shape, mybir.dt.from_np(arr.dtype), kind="ExternalInput").ap()
    out = nc.dram_tensor("out", (B, S, TD), F32, kind="ExternalOutput").ap()
    decoder_kernel(nc, t, out)
    r = run_bass_kernel_spmd(nc, [arrays], core_ids=[0])
    return r.results[0]["out"]
```

```python
from contextlib import ExitStack

import concourse.bass as bass
from concourse import mybir

F32 = mybir.dt.float32
F32R = mybir.dt.float32r
I32 = mybir.dt.int32
ALU = mybir.AluOpType
ACT = mybir.ActivationFunctionType

B, S, TD, SD = 4, 256, 128, 64
LAYERS, H, D, FF = 6, 16, 64, 512
P = 128
RT = S // P
PAIRS = H // 2
SELF = B * PAIRS
STEPS = 2 * SELF
LEAD = 3
CUT = PAIRS
MASKED = -float(2 ** 100)
EPS, EPS2 = 1e-5, 1e-6
SCALE = D ** -0.5
SCALE1 = TD ** -0.5

RESIDUAL = ("self_out", "cross_out", "mlp_down")
SPLIT = ("fold_a", "fold_q")


def next_layers(kind, b, c):
    return kind == "fold_a" or kind == "norm_self" and b < 2 or kind == "v" and (b == 0 or b == 1 and c < RT)


def body_fillers():
    out = []
    for b in range(B):
        for c in range(2 * RT):
            start = (STEPS if next_layers("v", b, c) else 0) + PAIRS * b + PAIRS // 2 * (c // RT)
            first = {0: 48, 1: 56 if c < RT else CUT, 2: 11, 3: 18}[b]
            out.append(("v", b, c, first, min(start, CUT + STEPS - 1)))
        end = PAIRS * (b + 1) + 1
        out.append(("norm_cross", b, 0, end + 2, end + 3))
        end = SELF + PAIRS * (b + 1) + 1
        out.append(("norm_mlp", b, 0, end + 2, end + 2))
        out += [("mlp_up", b, c, end + 3 + c, end + 3 + c) for c in range(2)]
        out.append(("mlp_down", b, 0, end + 5, end + 5))
        out.append(("norm_self", b, 0) + ((end + 7, end + 7) if b < 2 else (CUT + 1, PAIRS * b - LEAD - 2)))
    out += [("fold_q", 0, c, 10, 27) for c in range(2)] + [("fold_o", 0, c, 30, 33) for c in range(2)]
    out += [("fold_a", 0, c, 34, 59) for c in range(PAIRS // 2)]
    return out


def place(fillers, steps):
    plan, left = {}, list(fillers)
    for s in steps:
        can = [f for f in left if f[3] <= s]
        if can:
            f = min(can, key=lambda x: x[4])
            assert s <= f[4], (s, f)
            left.remove(f)
            plan[s] = f[:3]
    assert not left, left
    return plan


STEP_RANGE = range(CUT, CUT + STEPS)
PLAN = place(body_fillers(), STEP_RANGE)
START = [("fold_a", 0, c) for c in range(PAIRS // 2)] + [("norm_self", 0, 0)] + [("v", 0, c) for c in range(2 * RT)]
WARM_RANGE = range(STEPS, STEPS + CUT)
WARM = {STEPS + i: f for i, f in enumerate(
    [("norm_self", 1, 0)] + [("v", 1, c) for c in range(RT)])}
LAST = {s: f for s, f in PLAN.items() if not next_layers(*f)}
LAST_RANGE = range(CUT, max(LAST) + 1)
LAST.update(zip([s for s in LAST_RANGE if s > SELF + 1 and s not in LAST],
                [("context", b, net) for net in range(3) for b in range(B)]))
assert len([f for f in LAST.values() if f[0] == "context"]) == 3 * B
OUTS = {PAIRS * (b + 1) + 1 + (SELF if kind == "cross_out" else 0): (kind, b, 0)
        for kind in ("self_out", "cross_out") for b in range(B)}
NORMS = 3 * B
SPLIT_V = 27
SPLIT_UP = 22


class Segment:

    def __init__(self, layer, steps, plan, fillers_before, norms_before, adds_before, turns_before, folds_before):
        self.layer, self.steps, self.plan = layer, steps, plan
        self.order = [plan[s] for s in sorted(plan)]
        self.fillers_before, self.norms_before, self.adds_before = fillers_before, norms_before, adds_before
        self.turns_before, self.folds_before = turns_before, folds_before
        self.residual_at = {} if plan is WARM else {
            **OUTS, **{s: f for s, f in plan.items() if f[0] in RESIDUAL}}
        self.residual = [self.residual_at[s] for s in sorted(self.residual_at)]
        self.normed = [f for f in self.residual if plan is not LAST or f[0] != "mlp_down"]
        self.turns = [f for f in self.order if f[0].startswith("norm")]
        self.folds = [f for f in self.order if f[0] in SPLIT]

    def pair(self, s):
        return self.layer * STEPS + s

    def filler(self, f):
        return self.fillers_before + self.order.index(f)

    def adds(self, f):
        return self.adds_before + self.residual.index(f)

    def norm_of(self, f):
        return self.norms_before + self.normed.index(f)

    def outs(self, f):
        return self.layer * len(OUTS) + [OUTS[s] for s in sorted(OUTS)].index(f)

    def turn(self, f):
        return self.turns_before + self.turns.index(f)

    def fold(self, f):
        return self.folds_before + self.folds.index(f)

    def rows_ready(self, f):
        if self.plan is WARM:
            return f[1] + 1
        if f[0] == "norm_self" and f[1] >= 2:
            return self.norms_before
        source = {"norm_cross": "self_out", "norm_mlp": "cross_out", "norm_self": "mlp_down"}[f[0]]
        return self.norm_of((source, f[1], 0)) + 1

    def count(self, used, s, before, order):
        here = [order.index(f) for step, f in self.plan.items() if f in used and step < s]
        return before + max((i + 1 for i in here), default=0)

    def taken(self, used, s):
        return self.count(used, s, self.fillers_before, self.order)

    def turned(self, used, s):
        return self.count(used, s, self.turns_before, self.turns)


N_BODY, TURNS_BODY, FOLDS_BODY = len(PLAN), NORMS, PAIRS // 2 + 2
N_WARM = len(START) + len(WARM)


def warm_segment():
    return Segment(-1, WARM_RANGE, WARM, len(START), B, 0, 1, PAIRS // 2)


def body_segment(layer):
    return Segment(layer, STEP_RANGE, PLAN, layer * N_BODY + N_WARM, layer * NORMS + B, layer * NORMS,
                   layer * TURNS_BODY + 2, layer * FOLDS_BODY + PAIRS // 2)


def last_segment():
    n = LAYERS - 1
    return Segment(n, LAST_RANGE, LAST, n * N_BODY + N_WARM, n * NORMS + B, n * NORMS, n * TURNS_BODY + 2,
                   n * FOLDS_BODY + PAIRS // 2)


def wait(engine, semaphore, n):
    if not isinstance(n, int) or n > 0:
        engine.wait_ge(semaphore, n)


def wait_apart(engine, semaphore, n, passed):
    engine.wait_ge(semaphore, n)
    engine.sem_inc(passed, 1)


def decoder_kernel(nc, t, out):
    ctx = ExitStack()
    with ctx:
        def sb(name, shape, dt=F32):
            return ctx.enter_context(nc.sbuf_tensor(name, shape, dt))

        def sem(name):
            return ctx.enter_context(nc.semaphore(name))

        x = sb("x", [P, B, RT, TD])
        z = sb("z", [P, B, RT, TD])
        tnT = sb("tnT", [P, S])
        tn_hi = sb("tn_hi", [P, B, S], F32R)
        tn_lo = sb("tn_lo", [P, B, S], F32R)
        q_hi = sb("q_hi", [P, 4, 2, S], F32R)
        q_lo = sb("q_lo", [P, 4, 2, S], F32R)
        v = sb("v", [P, 2, RT, H * D])
        probs = sb("probs", [P, 4, RT, S])
        probsT = sb("probsT", [P, 4, RT, S])
        attT = sb("attT", [P, 2, S])
        neg_self = sb("neg_self", [P, B, RT, S])
        neg_cross = sb("neg_cross", [P, B, S])
        neg_none = sb("neg_none", [P, S])
        ident = sb("ident", [P, P])
        srcT = sb("srcT", [P, B, S])
        src_hi = sb("src_hi", [P, B, S], F32R)
        src_lo = sb("src_lo", [P, B, S], F32R)
        src = sb("src", [P, B, RT, SD])
        w_qT = sb("w_qT", [P, PAIRS, TD])
        w_kT = sb("w_kT", [P, PAIRS, 2 * TD])
        w_v = sb("w_v", [P, H * D])
        v_hi = sb("v_hi", [P, H * D], F32R)
        v_lo = sb("v_lo", [P, H * D], F32R)
        a_hi = sb("a_hi", [P, PAIRS, 2 * TD], F32R)
        a_lo = sb("a_lo", [P, PAIRS, 2 * TD], F32R)
        w_o = sb("w_o", [P, PAIRS, TD])
        cw = sb("cw", [P, 4, PAIRS, TD])
        cw_qT, cw_kT, cw_vT, cw_o = (cw[:, i] for i in range(4))
        c_hi = sb("c_hi", [P, PAIRS, 2 * SD], F32R)
        c_lo = sb("c_lo", [P, PAIRS, 2 * SD], F32R)
        fold_o = sb("fold_o", [P, PAIRS, TD])
        w_up = sb("w_up", [P, FF])
        up_hi = sb("up_hi", [P, FF], F32R)
        up_lo = sb("up_lo", [P, FF], F32R)
        w_down = sb("w_down", [P, FF // P, TD])
        b_up = sb("b_up", [P, FF // P])
        upT = sb("upT", [P, FF // P, S])
        rows = sb("rows", [P, 3, TD])
        norm_gb = sb("norm_gb", [P, 2])
        pre_gb = sb("pre_gb", [P, 2])
        min_u = sb("min_u", [P, 4, RT])
        row_sum = sb("row_sum", [P, 4, RT])
        row_inv = sb("row_inv", [P, 4, RT])
        bn = sb("bn", [P, RT, 6])
        mean_var = sb("mean_var", [P, RT, 2])
        var_eps = sb("var_eps", [P, RT])
        rstd = sb("rstd", [P, RT])
        minus_half = sb("minus_half", [P, RT])
        e_kT = sb("e_kT", [P, 3 * B, S])
        e_wq = sb("e_wq", [P, 3, TD])
        e_wk = sb("e_wk", [SD, 3, TD])
        e_wv = sb("e_wv", [SD, 3, TD])
        e_wo = sb("e_wo", [P, 2, TD])
        e_bqkv = sb("e_bqkv", [P, 3, 3])
        e_rows = sb("e_rows", [P, 5, TD])
        e_min = sb("e_min", [P, B, RT])
        e_sum = sb("e_sum", [P, B, RT])
        e_inv = sb("e_inv", [P, B, RT])
        e_bn = sb("e_bn", [P, B, RT, 6])
        e_mv = sb("e_mv", [P, B, RT, 2])
        e_ve = sb("e_ve", [P, B, RT])
        e_rstd = sb("e_rstd", [P, B, RT])
        part = lambda a, lo, n, m: a[:, lo:lo + n * m].rearrange("p (n m) -> p n m", m=m)
        cw_flat = cw[:, :, :, :].rearrange("p a b c -> p (a b c)")
        e_v = part(v[:, :, :, :].rearrange("p a b c -> p (a b c)"), 0, 3 * B * RT, TD)
        e_probs = part(w_kT[:, :, :].rearrange("p a b -> p (a b)"), 0, B * RT, S)
        e_probsT = part(cw_flat, 0, B * RT, S)
        e_xT = part(cw_flat, 2 * B * S, B, S)
        e_qT = part(cw_flat, 3 * B * S, B, S)
        e_aT = part(w_qT[:, :, :].rearrange("p a b -> p (a b)"), 0, B, S)

        scores = ctx.enter_context(nc.psum_tensor("scores", [P, 2, RT, S], F32))
        turned = ctx.enter_context(nc.psum_tensor("turned", [P, 2, RT, S], F32))
        att = ctx.enter_context(nc.psum_tensor("att", [P, 512], F32))
        out_ps = ctx.enter_context(nc.psum_tensor("out_ps", [P, 512], F32))
        q_ps = ctx.enter_context(nc.psum_tensor("q_ps", [P, 2, S], F32))
        proj = ctx.enter_context(nc.psum_tensor("proj", [P, 512], F32))
        halves = lambda a: a.rearrange("p (a b) -> p a b", a=RT)
        e_a = [turned[:, 0], turned[:, 1], halves(att[:, :]), halves(out_ps[:, :])]
        e_b = [scores[:, 0], scores[:, 1], q_ps[:, :, :], halves(proj[:, :])]

        x_loaded, consts_loaded, masks_loaded = sem("x_loaded"), sem("consts_loaded"), sem("masks_loaded")
        ctx_loaded, e_loaded = sem("ctx_loaded"), sem("e_loaded")
        self_loaded, attw_loaded, mlp_loaded = sem("self_loaded"), sem("attw_loaded"), sem("mlp_loaded")
        ident_zeroed, ident_ready = sem("ident_zeroed"), sem("ident_ready")
        blocks_zeroed, neg_ready = sem("blocks_zeroed"), sem("neg_ready")
        half_ready = sem("half_ready")
        scores_ready, turned_ready, att_ready, proj_ready = (
            sem("scores_ready"), sem("turned_ready"), sem("att_ready"), sem("proj_ready"))
        out_ready, out_taken = sem("out_ready"), sem("out_taken")
        proj_taken = sem("proj_taken")
        q_ready, q_hi_taken, q_taken = sem("q_ready"), sem("q_hi_taken"), sem("q_taken")
        fold_hi_taken = sem("fold_hi_taken")
        tn_ready = sem("tn_ready")
        v_hi_ready, v_split, up_hi_ready, up_split = sem("v_hi_ready"), sem("v_split"), sem("up_hi_ready"), sem("up_split")
        src_hi_ready, src_split = sem("src_hi_ready"), sem("src_split")
        shifted = sem("shifted")
        exp_done, inv_ready, probs_ready = sem("exp_done"), sem("inv_ready"), sem("probs_ready")
        turned_taken, att_taken = sem("turned_taken"), sem("att_taken")
        bn_ready, mv_ready, var_ready, rstd_ready, z_ready = (
            sem("bn_ready"), sem("mv_ready"), sem("var_ready"), sem("rstd_ready"), sem("z_ready"))
        bias_added = sem("bias_added")
        waits_passed = sem("waits_passed")
        E = {n: sem("e_" + n) for n in (
            "biased", "xT_ps", "xT", "q_ps", "q", "s_ps", "shifted", "exp", "inv", "norm",
            "pT_ps", "pT", "a_ps", "a", "o_ps", "x", "bn", "mv", "var", "rstd", "z", "zg")}
        stored = sem("stored")

        SELF_DMAS, ATTW_DMAS, MLP_DMAS = 4, 8, 7
        pairs = "(c r) m -> r c m"

        def blocks(q, w, kvT, first, size, loaded):
            heads = kvT[first:first + H * D].rearrange("(c h r) m -> h r c m", h=2, r=D)
            for j in range(2):
                q.dma_start(w[j * D:(j + 1) * D, :, j * size:(j + 1) * size], heads[j]).then_inc(loaded, 16)

        def load_self(q, l):
            q.dma_start(w_qT[:, :, :], t["sa_qT"][l].rearrange(pairs, r=P)).then_inc(self_loaded, 16)
            blocks(q, w_kT, t["sa_kT"][l], 0, TD, self_loaded)
            q.dma_start(w_v[:, :], t["sa_kv"][l][:, H * D:2 * H * D]).then_inc(self_loaded, 16)

        def load_attw(q, l):
            row = t["sa_ob"][l:l + 1, :] if isinstance(l, int) else t["sa_ob"][bass.ds(l, 1), :]
            q.dma_start(w_o[:, :, :], t["sa_ow"][l].rearrange(pairs, r=P)).then_inc(attw_loaded, 16)
            q.dma_start(rows[:, 0, :], row.partition_broadcast(P)).then_inc(attw_loaded, 16)
            q.dma_start(cw_qT, t["ca_qT"][l].rearrange(pairs, r=P)).then_inc(attw_loaded, 16)
            q.dma_start(cw_o, t["ca_ow"][l].rearrange(pairs, r=P)).then_inc(attw_loaded, 16)
            blocks(q, cw_kT, t["ca_kvT"][l], 0, SD, attw_loaded)
            blocks(q, cw_vT, t["ca_kvT"][l], H * D, SD, attw_loaded)

        def load_mlp(q, l):
            row = (lambda n: t[n][l:l + 1, :]) if isinstance(l, int) else (lambda n: t[n][bass.ds(l, 1), :])
            q.dma_start(w_up[:, :], t["ff_w1"][l]).then_inc(mlp_loaded, 16)
            q.dma_start(w_down[:, :, :], t["ff_w2"][l].rearrange("(c r) m -> r c m", r=P)).then_inc(mlp_loaded, 16)
            q.dma_start(b_up[:, :], row("ff_b1").rearrange("a (c r) -> r (a c)", r=P)).then_inc(mlp_loaded, 16)
            q.dma_start(rows[:, 1, :], row("ca_ob").partition_broadcast(P)).then_inc(mlp_loaded, 16)
            q.dma_start(rows[:, 2, :], row("ff_b2").partition_broadcast(P)).then_inc(mlp_loaded, 16)
            q.dma_start(pre_gb[:, 0:1], row("pre_g").rearrange("a r -> r a")).then_inc(mlp_loaded, 16)
            q.dma_start(pre_gb[:, 1:2], row("pre_b").rearrange("a r -> r a")).then_inc(mlp_loaded, 16)

        ctx.enter_context(nc.allow_non_contiguous_dma("biases and gains onto partitions"))
        block = ctx.enter_context(nc.Block())

        @block.sync
        def _(sp):
            sp.dma_start(x[:, :, :, :], t["x"].rearrange("b (r p) d -> p b r d", p=P)).then_inc(x_loaded, 16)
            col = lambda n: t[n].rearrange("(r a) -> r a", a=1)
            sp.dma_start(norm_gb[:, 0:1], col("norm_g")).then_inc(consts_loaded, 16)
            sp.dma_start(norm_gb[:, 1:2], col("norm_b")).then_inc(consts_loaded, 16)
            sp.wait_ge(blocks_zeroed, 3)
            load_self(sp, 0)
            sp.dma_start(neg_self[:, :, :, :].bitcast(I32),
                         t["mask_self"].rearrange("b (r p) k -> p b r k", p=P)).then_inc(masks_loaded, 16)
            sp.dma_start(neg_cross[:, :, :].bitcast(I32).rearrange("p b k -> p (b k)"),
                         t["mask_cross"].rearrange("b a k -> a (b k)").partition_broadcast(P)).then_inc(masks_loaded, 16)
            for j in range(2):
                sp.dma_start(srcT[j * SD:(j + 1) * SD, :, :], t["srcT"][:, :, :]).then_inc(ctx_loaded, 16)
            sp.dma_start(src[:, :, :, :], t["ctx"].rearrange("b (r p) d -> p b r d", p=P)).then_inc(ctx_loaded, 16)
            load_attw(sp, 0)
            load_mlp(sp, 0)
            for n, name in enumerate(("L1", "L2", "L3")):
                sp.dma_start(e_wq[:, n, :], t[name + "_Wq"]).then_inc(e_loaded, 16)
                sp.dma_start(e_wk[:, n, :], t[name + "_Wk"]).then_inc(e_loaded, 16)
                sp.dma_start(e_wv[:, n, :], t[name + "_Wv"]).then_inc(e_loaded, 16)
                for i, bias in enumerate(("_bq", "_bk", "_bv")):
                    sp.dma_start(e_bqkv[:, n, i:i + 1], col(name + bias)).then_inc(e_loaded, 16)
            sp.dma_start(e_wo[:, 0, :], t["L1_Wo"]).then_inc(e_loaded, 16)
            sp.dma_start(e_wo[:, 1, :], t["L3_Wo"]).then_inc(e_loaded, 16)
            for i, name in enumerate(("L1_bo", "L3_bo", "L2_bv", "L2_gamma", "L2_beta")):
                sp.dma_start(e_rows[:, i, :], t[name].rearrange("(a n) -> a n", a=1).partition_broadcast(P)
                             ).then_inc(e_loaded, 16)
            with sp.Fori(0, LAYERS - 1) as l:
                seg = body_segment(l)
                wait_apart(sp, scores_ready, 2 * seg.pair(10), waits_passed)
                load_self(sp, l + 1)
                wait_apart(sp, scores_ready, 2 * seg.pair(41), waits_passed)
                wait_apart(sp, bias_added, seg.adds_before + B, waits_passed)
                load_attw(sp, l + 1)
                wait_apart(sp, scores_ready, 2 * seg.pair(73), waits_passed)
                wait_apart(sp, bias_added, seg.adds_before + NORMS, waits_passed)
                load_mlp(sp, l + 1)
            for b in range(B):
                sp.wait_ge(E["x"], 2 * B + b + 1)
                sp.dma_start(out[b].rearrange("(r p) d -> p r d", p=P), x[:, b]).then_inc(stored, 16)
            sp.wait_ge(stored, 16 * B)

        E_DMAS = 3 * 6 + 2 + 5

        @block.tensor
        def _(pe):
            def head_scores(seg, s, j):
                layer_s = s % STEPS
                cross, b, c = layer_s >= SELF, layer_s % SELF // PAIRS, layer_s % PAIRS
                if j == 0:
                    pe.wait_ge(q_taken, seg.pair(s) + 1)
                wait(pe, exp_done, (seg.pair(s) - 1) * 2 + j + 1)
                for r in range(RT):
                    at = slice(r * P, (r + 1) * P)
                    hi, lo = q_hi[:, s % 4, j, at], q_lo[:, s % 4, j, at]
                    passes = [(hi, src_hi), (hi, src_lo)] if cross else [(hi, tn_hi), (hi, tn_lo), (lo, tn_hi)]
                    for i, (q, k) in enumerate(passes):
                        mm = nc.tensor.matmul(scores[:, j, r, :], q, k[:, b, :],
                                              start=(i == 0), stop=(i == len(passes) - 1))
                mm.then_inc(scores_ready, 1)

            def queries(seg, s, waited=False):
                layer_s = s % STEPS
                cross, b, c = layer_s >= SELF, layer_s % SELF // PAIRS, layer_s % PAIRS
                wait(pe, q_taken, seg.pair(s))
                if c == 0 and not waited:
                    kind = "norm_cross" if cross else "norm_self"
                    pe.wait_ge(tn_ready, seg.turned([(kind, b, 0)], s - LEAD))
                    if b == 0:
                        folds = [("fold_q", 0, i) for i in range(2)] if cross else [
                            ("fold_a", 0, i) for i in range(PAIRS // 2)]
                        pe.wait_ge(proj_taken, seg.taken(folds, s - LEAD))
                for j in range(1 if cross else 2):
                    w_hi, w_lo = (c_hi[:, c, :], c_lo[:, c, :]) if cross else (
                        w[:, c, j * TD:(j + 1) * TD] for w in (a_hi, a_lo))
                    for i, (w, tn) in enumerate(((w_hi, tn_hi), (w_hi, tn_lo), (w_lo, tn_hi))):
                        mm = nc.tensor.matmul(q_ps[:, j, :], w, tn[:, b, :], start=(i == 0), stop=(i == 2))
                mm.then_inc(q_ready, 1)

            def pair_turn(seg, s, j):
                pe.wait_ge(probs_ready, seg.pair(s) * 2 + j + 1)
                wait(pe, turned_taken, (seg.pair(s) - 1) * 2 + j + 1)
                for k in range(RT):
                    for r in range(RT):
                        mm = nc.tensor.transpose(turned[:, j, k, r * P:(r + 1) * P],
                                                 probs[:, 2 * (s % 2) + j, r, k * P:(k + 1) * P], ident[:, :])
                mm.then_inc(turned_ready, 1)

            def pair_values(seg, s):
                layer_s = s % STEPS
                cross, b, c = layer_s >= SELF, layer_s % SELF // PAIRS, layer_s % PAIRS
                pe.wait_ge(turned_taken, (seg.pair(s) + 1) * 2)
                wait(pe, att_taken, seg.pair(s))
                if not cross and c % (PAIRS // 2) == 0:
                    half = c // (PAIRS // 2)
                    pe.wait_ge(proj_taken, seg.taken([("v", b, half * RT + i) for i in range(RT)], s + 1))
                for k in range(RT):
                    for j in range(2):
                        val = src[:, b, k, :] if cross else v[:, b % 2, k, (2 * c + j) * D:(2 * c + j + 1) * D]
                        mm = nc.tensor.matmul(att[j * D:(j + 1) * D, 0:S], val, probsT[:, 2 * (s % 2) + j, k, :],
                                              start=(k == 0), stop=(k == RT - 1))
                mm.then_inc(att_ready, 1)

            def output(seg, s):
                layer_s = s % STEPS
                cross, c = layer_s >= SELF, layer_s % PAIRS
                pe.wait_ge(att_taken, seg.pair(s) + 1)
                if c == 0:
                    wait(pe, out_taken, seg.layer * len(OUTS) + s // PAIRS)
                    if not cross:
                        pe.wait_ge(attw_loaded, 16 * ATTW_DMAS * (seg.layer + s // STEPS + 1))
                w = fold_o if cross else w_o
                for r in range(RT):
                    mm = nc.tensor.matmul(out_ps[:, r * P:(r + 1) * P], attT[:, s % 2, r * P:(r + 1) * P], w[:, c, :],
                                          start=(c == 0 and r == 0), stop=(c == PAIRS - 1 and r == RT - 1))
                if c == PAIRS - 1:
                    mm.then_inc(out_ready, 1)

            def filler(seg, f, weights):
                kind, b, c = f
                n = seg if isinstance(seg, int) else seg.filler(f)
                wait(pe, proj_taken, n)
                if kind in ("norm_self", "norm_cross", "norm_mlp"):
                    pe.wait_ge(z_ready, weights)
                    for r in range(RT):
                        mm = nc.tensor.transpose(proj[:, r * P:(r + 1) * P], z[:, b, r, :], ident[:, :])
                elif kind == "v":
                    half, r = c // RT, c % RT
                    if weights is not None:
                        pe.wait_ge(v_split, weights[0])
                        pe.wait_ge(tn_ready, weights[1])
                    rows_at, cols = slice(r * P, (r + 1) * P), slice(half * 512, (half + 1) * 512)
                    for i, (tn, w) in enumerate(((tn_hi, v_hi), (tn_hi, v_lo), (tn_lo, v_hi))):
                        mm = nc.tensor.matmul(proj[:, :], tn[:, b, rows_at], w[:, cols], start=(i == 0), stop=(i == 2))
                elif kind == "fold_a":
                    pe.wait_ge(self_loaded, weights)
                    for i in range(2):
                        mm = nc.tensor.matmul(proj[:, i * S:(i + 1) * S], w_qT[:, 2 * c + i, :], w_kT[:, 2 * c + i, :],
                                              start=True, stop=True)
                elif kind == "fold_q":
                    pe.wait_ge(attw_loaded, weights)
                    for i in range(4):
                        mm = nc.tensor.matmul(proj[:, i * P:(i + 1) * P], cw_qT[:, 4 * c + i, :],
                                              cw_kT[:, 4 * c + i, :], start=True, stop=True)
                elif kind == "fold_o":
                    pe.wait_ge(attw_loaded, weights)
                    for i in range(4):
                        mm = nc.tensor.matmul(proj[:, i * P:(i + 1) * P], cw_vT[:, 4 * c + i, :],
                                              cw_o[:, 4 * c + i, :], start=True, stop=True)
                elif kind == "context":
                    if weights:
                        pe.wait_ge(e_loaded, weights)
                    nc.tensor.matmul(proj[:, 0:S], e_wk[:, c, :], srcT[0:SD, b, :], start=True, stop=True)
                    for r in range(RT):
                        mm = nc.tensor.matmul(proj[:, S + r * P:S + (r + 1) * P], srcT[0:SD, b, r * P:(r + 1) * P],
                                              e_wv[:, c, :], start=True, stop=True)
                elif kind == "mlp_up":
                    pe.wait_ge(up_split, weights[0])
                    pe.wait_ge(tn_ready, weights[1])
                    for j in range(2):
                        cols = slice((2 * c + j) * P, (2 * c + j + 1) * P)
                        for i, (w, tn) in enumerate(((up_hi, tn_hi), (up_hi, tn_lo), (up_lo, tn_hi))):
                            mm = nc.tensor.matmul(proj[:, j * S:(j + 1) * S], w[:, cols], tn[:, b, :],
                                                  start=(i == 0), stop=(i == 2))
                elif kind == "mlp_down":
                    for r in range(RT):
                        for i in range(FF // P):
                            mm = nc.tensor.matmul(proj[:, r * P:(r + 1) * P], upT[:, i, r * P:(r + 1) * P],
                                                  w_down[:, i, :], start=(i == 0), stop=(i == FF // P - 1))
                mm.then_inc(proj_ready, 1)

            def weights_of(seg, s, f):
                kind, b, c = f
                if kind.startswith("norm"):
                    return seg.rows_ready(f)
                if kind == "v":
                    return (seg.layer + (2 if next_layers(*f) else 1), seg.turned([("norm_self", b, 0)], s)) if c == 0 else None
                if kind == "fold_a":
                    return 16 * SELF_DMAS * (seg.layer + 2)
                if kind == "context":
                    return 16 * E_DMAS if b == c == 0 else None
                if kind.startswith("fold"):
                    return 16 * ATTW_DMAS * (seg.layer + 1)
                if kind == "mlp_up":
                    return seg.layer + 1, seg.turned([("norm_mlp", b, 0)], s)
                return None

            def steps(seg, final=False):
                for s in seg.steps:
                    if not (final and s >= STEPS - 1):
                        head_scores(seg, s + 1, 0)
                        head_scores(seg, s + 1, 1)
                    if not (final and s >= STEPS - LEAD):
                        queries(seg, s + LEAD)
                    if not (final and s > STEPS + 1) and not (seg.plan is WARM and s < STEPS + 2):
                        output(seg, s - 2)
                    if not (final and s >= STEPS):
                        pair_turn(seg, s, 0)
                        pair_turn(seg, s, 1)
                    if s in seg.plan:
                        filler(seg, seg.plan[s], weights_of(seg, s, seg.plan[s]))
                    if not (final and s > STEPS) and not (seg.plan is WARM and s == STEPS):
                        pair_values(seg, s - 1)

            pe.wait_ge(ident_ready, 1)
            first = warm_segment()
            start_needs = {"fold_a": 16 * SELF_DMAS, "norm_self": 1, "v": (1, 1)}
            for n, f in enumerate(START):
                filler(n, f, start_needs[f[0]])
                if f[0] == "norm_self":
                    pe.wait_ge(proj_taken, n)
                    pe.wait_ge(tn_ready, 1)
                    for p in range(LEAD):
                        queries(first, STEPS + p, waited=True)
            head_scores(first, STEPS, 0)
            head_scores(first, STEPS, 1)
            steps(first)
            pe.wait_ge(ctx_loaded, 16 * 3)
            pe.wait_ge(src_split, 1)
            with pe.Fori(0, LAYERS - 1) as l:
                steps(body_segment(l))
            steps(last_segment(), final=True)

            pe.wait_ge(proj_taken, N_WARM + (LAYERS - 1) * N_BODY + len(LAST))
            for net in range(3):
                for b in range(B):
                    if net:
                        pe.wait_ge(E["x"], (net - 1) * B + b + 1)
                    for r in range(RT):
                        mm = nc.tensor.transpose(e_a[b][:, 0, r * P:(r + 1) * P], x[:, b, r, :], ident[:, :])
                    mm.then_inc(E["xT_ps"], 1)
                for b in range(B):
                    pe.wait_ge(E["xT"], net * B + b + 1)
                    nc.tensor.matmul(e_a[b][:, 0, :], e_wq[:, net, :], e_xT[:, b, :], start=True, stop=True
                                     ).then_inc(E["q_ps"], 1)
                for b in range(B):
                    pe.wait_ge(E["q"], net * B + b + 1)
                    for r in range(RT):
                        at = slice(r * P, (r + 1) * P)
                        lhs, rhs = (e_kT[:, B + b, at], e_qT[:, b, :]) if net == 1 else (
                            e_qT[:, b, at], e_kT[:, net * B + b, :])
                        mm = nc.tensor.matmul(e_b[b][:, r, :], lhs, rhs, start=True, stop=True)
                    mm.then_inc(E["s_ps"], 1)
                if net == 1:
                    for b in range(B):
                        pe.wait_ge(E["norm"], B + b + 1)
                        for r in range(RT):
                            for k in range(RT):
                                mm = nc.tensor.matmul(e_a[b][:, 0, r * P:(r + 1) * P],
                                                      e_probs[:, b * RT + k, r * P:(r + 1) * P],
                                                      e_v[:, (B + b) * RT + k, :], start=(k == 0), stop=(k == RT - 1))
                        mm.then_inc(E["o_ps"], 1)
                    continue
                m = 0 if net == 0 else 1
                for b in range(B):
                    pe.wait_ge(E["norm"], net * B + b + 1)
                    for k in range(RT):
                        for r in range(RT):
                            mm = nc.tensor.transpose(e_a[b][:, k, r * P:(r + 1) * P],
                                                     e_probs[:, b * RT + r, k * P:(k + 1) * P], ident[:, :])
                    mm.then_inc(E["pT_ps"], 1)
                for b in range(B):
                    pe.wait_ge(E["pT"], m * B + b + 1)
                    for k in range(RT):
                        mm = nc.tensor.matmul(e_b[b][:, 0, :], e_v[:, (net * B + b) * RT + k, :],
                                              e_probsT[:, b * RT + k, :], start=(k == 0), stop=(k == RT - 1))
                    mm.then_inc(E["a_ps"], 1)
                for b in range(B):
                    pe.wait_ge(E["a"], m * B + b + 1)
                    for r in range(RT):
                        mm = nc.tensor.matmul(e_a[b][:, 0, r * P:(r + 1) * P], e_aT[:, b, r * P:(r + 1) * P],
                                              e_wo[:, m, :], start=True, stop=True)
                    mm.then_inc(E["o_ps"], 1)

        @block.scalar
        def _(act):
            def exps(seg, s, j):
                act.wait_ge(shifted, seg.pair(s) * 2 + j + 1)
                slot = 2 * (s % 2) + j
                for r in range(RT):
                    e = nc.scalar.activation(probs[:, slot, r, :], scores[:, j, r, :], ACT.Exp,
                                             bias=min_u[:, slot, r:r + 1], scale=-1.0,
                                             accum_out=row_sum[:, slot, r:r + 1])
                e.then_inc(exp_done, 1)

            def take_att(seg, s):
                act.wait_ge(att_ready, seg.pair(s) + 1)
                nc.scalar.activation(attT[:, s % 2, :], att[:, 0:S], ACT.Copy).then_inc(att_taken, 1)

            def take_q(seg, s):
                act.wait_ge(q_ready, seg.pair(s) + 1)
                if s % STEPS >= SELF:
                    for j in range(2):
                        a = nc.scalar.activation(q_hi[0:SD, s % 4, j, :], q_ps[j * SD:(j + 1) * SD, 0, :], ACT.Copy)
                else:
                    a = nc.scalar.activation(q_hi[:, s % 4, :, :], q_ps[:, :, :], ACT.Copy)
                a.then_inc(q_hi_taken, 1)

            def take(n, f, layer):
                kind, b, c = f
                act.wait_ge(proj_ready, n + 1)
                quarters = proj[:, :].rearrange("p (a b) -> p a b", a=4)
                if kind.startswith("norm"):
                    if kind == "norm_mlp":
                        act.wait_ge(mlp_loaded, 16 * MLP_DMAS * (layer + 1))
                    gb = pre_gb if kind == "norm_mlp" else norm_gb
                    for dst in (tnT[:, :], tn_hi[:, b, :]):
                        a = nc.scalar.activation(dst, proj[:, 0:S], ACT.Identity, scale=gb[:, 0:1], bias=gb[:, 1:2])
                    a.then_inc(proj_taken, 1)
                elif kind == "mlp_up":
                    for i in range(2):
                        a = nc.scalar.activation(upT[:, 2 * c + i, :], proj[:, i * S:(i + 1) * S], ACT.Relu,
                                                 bias=b_up[:, 2 * c + i:2 * c + i + 1])
                    a.then_inc(proj_taken, 1)
                elif kind == "fold_a":
                    nc.scalar.activation(a_hi[:, 2 * c:2 * c + 2, :], halves(proj[:, :]), ACT.Copy
                                         ).then_inc(fold_hi_taken, 1)
                elif kind == "fold_q":
                    nc.scalar.activation(c_hi[:, 4 * c:4 * c + 4, :], quarters, ACT.Copy).then_inc(fold_hi_taken, 1)
                elif kind == "context":
                    nc.scalar.activation(e_kT[:, c * B + b, :], proj[:, 0:S], ACT.Identity, bias=e_bqkv[:, c, 1:2])
                    nc.scalar.activation(e_v[:, (c * B + b) * RT:(c * B + b + 1) * RT, :], halves(proj[:, :])[:, 1, :],
                                         ACT.Copy).then_inc(proj_taken, 1)
                elif kind == "fold_o":
                    nc.scalar.activation(fold_o[:, 4 * c:4 * c + 4, :], quarters, ACT.Copy).then_inc(proj_taken, 1)
                elif kind == "v":
                    nc.scalar.activation(v[:, b % 2, c % RT, (c // RT) * 512:(c // RT + 1) * 512], proj[:, :],
                                         ACT.Copy).then_inc(proj_taken, 1)

            def steps(seg, final=False):
                for s in seg.steps:
                    if s > seg.steps[0] and not (final and s > STEPS + 1) and not (seg.plan is WARM and s == STEPS + 1):
                        take_att(seg, s - 2)
                    heads = not (final and s >= STEPS - 1)
                    if heads:
                        exps(seg, s + 1, 0)
                    if not (final and s >= STEPS - LEAD):
                        take_q(seg, s + LEAD)
                    if heads:
                        exps(seg, s + 1, 1)
                    if s in seg.plan and seg.plan[s][0] not in RESIDUAL:
                        take(seg.filler(seg.plan[s]), seg.plan[s], seg.layer)
                if not final:
                    take_att(seg, seg.steps[-1] - 1)

            act.wait_ge(consts_loaded, 32)
            for n, f in enumerate(START):
                take(n, f, 0)
                if f[0] == "norm_self":
                    for p in range(LEAD):
                        take_q(warm_segment(), STEPS + p)
            seg = warm_segment()
            exps(seg, STEPS, 0)
            exps(seg, STEPS, 1)
            steps(seg)
            with act.Fori(0, LAYERS - 1) as l:
                steps(body_segment(l))
            steps(last_segment(), final=True)

            for net in range(3):
                for b in range(B):
                    act.wait_ge(E["xT_ps"], net * B + b + 1)
                    nc.scalar.activation(e_xT[:, b, :], e_a[b][:, 0, :], ACT.Copy).then_inc(E["xT"], 1)
                for b in range(B):
                    act.wait_ge(E["q_ps"], net * B + b + 1)
                    nc.scalar.activation(e_qT[:, b, :], e_a[b][:, 0, :], ACT.Identity, bias=e_bqkv[:, net, 0:1]
                                         ).then_inc(E["q"], 1)
                for b in range(B):
                    act.wait_ge(E["shifted"], net * B + b + 1)
                    for r in range(RT):
                        e = nc.scalar.activation(e_probs[:, b * RT + r, :], e_b[b][:, r, :], ACT.Exp,
                                                 bias=e_min[:, b, r:r + 1], scale=-1.0, accum_out=e_sum[:, b, r:r + 1])
                    e.then_inc(E["exp"], 1)
                if net == 1:
                    continue
                m = 0 if net == 0 else 1
                for b in range(B):
                    act.wait_ge(E["pT_ps"], m * B + b + 1)
                    nc.scalar.activation(e_probsT[:, b * RT:(b + 1) * RT, :], e_a[b], ACT.Copy).then_inc(E["pT"], 1)
                for b in range(B):
                    act.wait_ge(E["a_ps"], m * B + b + 1)
                    nc.scalar.activation(e_aT[:, b, :], e_b[b][:, 0, :], ACT.Identity, bias=e_bqkv[:, net, 2:3]
                                         ).then_inc(E["a"], 1)

        @block.vector
        def _(dve):
            def shift(seg, s, j):
                layer_s = s % STEPS
                cross, b = layer_s >= SELF, layer_s % SELF // PAIRS
                slot = 2 * (s % 2) + j
                wait_apart(dve, scores_ready, seg.pair(s) * 2 + j + 1, waits_passed)
                for r in range(RT):
                    d = nc.vector.tensor_tensor_reduce(
                        out=scores[:, j, r, :], in0=scores[:, j, r, :],
                        in1=neg_cross[:, b, :] if cross else neg_self[:, b, r, :], scale=-SCALE, scalar=3e38,
                        op0=ALU.add, op1=ALU.min, accum_out=min_u[:, slot, r:r + 1])
                d.then_inc(shifted, 1)

            def invert(seg, s, j):
                slot = 2 * (s % 2) + j
                dve.wait_ge(exp_done, seg.pair(s) * 2 + j + 1)
                nc.vector.reciprocal(row_inv[:, slot, :], row_sum[:, slot, :]).then_inc(inv_ready, 1)

            def take_turned(seg, s, j):
                dve.wait_ge(turned_ready, seg.pair(s) * 2 + j + 1)
                nc.vector.tensor_copy(probsT[:, 2 * (s % 2) + j, :, :], turned[:, j, :, :]).then_inc(turned_taken, 1)

            def take_q(seg, s):
                dve.wait_ge(q_hi_taken, seg.pair(s) + 1)
                if s % STEPS >= SELF:
                    for j in range(2):
                        d = nc.vector.tensor_tensor(q_hi[SD:P, s % 4, j, :], q_ps[j * SD:(j + 1) * SD, 0, :],
                                                    q_hi[0:SD, s % 4, j, :].bitcast(F32), ALU.subtract)
                else:
                    d = nc.vector.tensor_tensor(q_lo[:, s % 4, :, :], q_ps[:, :, :], q_hi[:, s % 4, :, :].bitcast(F32),
                                                ALU.subtract)
                d.then_inc(q_taken, 1)

            def split_fold(n_fold, f):
                kind, _, c = f
                dve.wait_ge(fold_hi_taken, n_fold + 1)
                if kind == "fold_a":
                    at, hi, lo, ps = slice(2 * c, 2 * c + 2), a_hi, a_lo, halves(proj[:, :])
                else:
                    at, hi, lo, ps = slice(4 * c, 4 * c + 4), c_hi, c_lo, proj[:, :].rearrange("p (a b) -> p a b", a=4)
                nc.vector.tensor_tensor(lo[:, at, :], ps, hi[:, at, :].bitcast(F32), ALU.subtract
                                        ).then_inc(proj_taken, 1)

            def split(whole, hi, lo, hi_ready, ready, n):
                nc.vector.tensor_copy(hi, whole).then_inc(hi_ready, 1)
                dve.wait_ge(hi_ready, n + 1)
                d = nc.vector.tensor_tensor(lo, whole, hi.bitcast(F32), ALU.subtract)
                if ready is not None:
                    d.then_inc(ready, 1)

            def split_v(part, layer):
                if part == 0:
                    dve.wait_ge(self_loaded, 16 * SELF_DMAS * (layer + 1))
                at = slice(part * 256, (part + 1) * 256)
                split(w_v[:, at], v_hi[:, at], v_lo[:, at], v_hi_ready, v_split if part == 3 else None, 4 * layer + part)

            def split_up(part, layer):
                if part == 0:
                    dve.wait_ge(mlp_loaded, 16 * MLP_DMAS * (layer + 1))
                at = slice(part * 256, (part + 1) * 256)
                split(w_up[:, at], up_hi[:, at], up_lo[:, at], up_hi_ready, up_split if part == 1 else None,
                      2 * layer + part)

            def stats(b, n):
                wait(dve, z_ready, n)
                for r in range(RT):
                    d = nc.vector.bn_stats(bn[:, r, :], x[:, b, r, :])
                d.then_inc(bn_ready, 1)
                wait_apart(dve, bn_ready, n + 1, waits_passed)
                for r in range(RT):
                    d = nc.vector.bn_aggr(mean_var[:, r, :], bn[:, r, :])
                d.then_inc(mv_ready, 1)
                dve.wait_ge(mv_ready, n + 1)
                nc.vector.tensor_scalar(var_eps[:, :], mean_var[:, :, 1], EPS, None, ALU.add).then_inc(var_ready, 1)

            def add(seg, f):
                if f[0] == "mlp_down":
                    ready, taken, n, bank = proj_ready, proj_taken, seg.filler(f), proj
                else:
                    ready, taken, n, bank = out_ready, out_taken, seg.outs(f), out_ps
                dve.wait_ge(ready, n + 1)
                dve.wait_ge(bias_added, seg.adds(f) + 1)
                nc.vector.tensor_tensor(x[:, f[1]], halves(bank[:, 0:S]), x[:, f[1]], ALU.add).then_inc(taken, 1)
                if f in seg.normed:
                    dve.wait_ge(taken, n + 1)
                    stats(f[1], seg.norm_of(f))

            def steps(seg, final=False):
                for s in seg.steps:
                    heads = not (final and s >= STEPS - 1)
                    turns = not (final and s >= STEPS)
                    f = seg.plan.get(s, ("",))
                    if heads:
                        shift(seg, s + 1, 0)
                        shift(seg, s + 1, 1)
                    if turns:
                        take_turned(seg, s, 0)
                    if heads:
                        invert(seg, s + 1, 0)
                    if turns:
                        take_turned(seg, s, 1)
                    if not (final and s >= STEPS - LEAD):
                        take_q(seg, s + LEAD)
                    if heads:
                        invert(seg, s + 1, 1)
                    if f[0] in SPLIT:
                        split_fold(seg.fold(f), f)
                    if seg.plan is PLAN and s - SPLIT_V in range(4):
                        split_v(s - SPLIT_V, seg.layer + 1)
                    if s - SPLIT_UP in range(2):
                        split_up(s - SPLIT_UP, seg.layer)
                    if s in seg.residual_at:
                        add(seg, seg.residual_at[s])

            nc.vector.memset(minus_half[:, :], -0.5).then_inc(half_ready, 1)
            for w in (w_kT[:, :, :], cw_kT, cw_vT):
                nc.vector.memset(w, 0.0).then_inc(blocks_zeroed, 1)
            dve.wait_ge(x_loaded, 16)
            stats(0, 0)
            seg = warm_segment()
            for n, f in enumerate(START):
                if f[0] == "fold_a":
                    split_fold(n, f)
                if f[0] == "norm_self":
                    for p in range(LEAD):
                        take_q(seg, STEPS + p)
            for i in range(4):
                split_v(i, 0)
            for b in range(1, B):
                stats(b, b)
            dve.wait_ge(masks_loaded, 32)
            for m in (neg_self[:, :, :, :].rearrange("p a b c -> p (a b c)"), neg_cross[:, :, :].rearrange("p a b -> p (a b)")):
                nc.vector.tensor_scalar(m, m.bitcast(I32), 0, MASKED, ALU.is_equal, ALU.mult).then_inc(neg_ready, 1)
            nc.vector.memset(neg_none[:, :], 0.0).then_inc(neg_ready, 1)
            dve.wait_ge(neg_ready, 3)
            for j in range(2):
                shift(seg, STEPS, j)
            for j in range(2):
                invert(seg, STEPS, j)
            dve.wait_ge(ctx_loaded, 16 * 3)
            split(srcT[:, :, :], src_hi[:, :, :], src_lo[:, :, :], src_hi_ready, src_split, 0)
            steps(seg)
            with dve.Fori(0, LAYERS - 1) as l:
                steps(body_segment(l))
            steps(last_segment(), final=True)

            dve.wait_ge(e_loaded, 16 * E_DMAS)
            dve.wait_ge(proj_taken, N_WARM + (LAYERS - 1) * N_BODY + len(LAST))
            for n in range(B, 2 * B):
                for r in range(RT):
                    nc.vector.tensor_tensor(e_v[:, n * RT + r, :], e_v[:, n * RT + r, :], e_rows[:, 2, :], ALU.add)
            for net in range(3):
                for b in range(B):
                    dve.wait_ge(E["s_ps"], net * B + b + 1)
                    for r in range(RT):
                        d = nc.vector.tensor_tensor_reduce(
                            out=e_b[b][:, r, :], in0=e_b[b][:, r, :], in1=neg_none[:, :], scale=-SCALE1, scalar=3e38,
                            op0=ALU.add, op1=ALU.min, accum_out=e_min[:, b, r:r + 1])
                    d.then_inc(E["shifted"], 1)
                for b in range(B):
                    dve.wait_ge(E["exp"], net * B + b + 1)
                    nc.vector.reciprocal(e_inv[:, b, :], e_sum[:, b, :]).then_inc(E["inv"], 1)
                for b in range(B):
                    dve.wait_ge(E["inv"], net * B + b + 1)
                    for r in range(RT):
                        d = nc.vector.tensor_scalar(e_probs[:, b * RT + r, :], e_probs[:, b * RT + r, :],
                                                    e_inv[:, b, r:r + 1], None, ALU.mult)
                    d.then_inc(E["norm"], 1)
                for b in range(B):
                    dve.wait_ge(E["o_ps"], net * B + b + 1)
                    if net != 1:
                        dve.wait_ge(E["biased"], (B if net == 2 else 0) + b + 1)
                    d = nc.vector.tensor_tensor(x[:, b], e_a[b][:, 0, :].rearrange("p (a b) -> p a b", a=RT), x[:, b],
                                                ALU.add)
                    d.then_inc(E["z"] if net == 1 else E["x"], 1)
                if net != 1:
                    continue
                for b in range(B):
                    dve.wait_ge(E["z"], b + 1)
                    for r in range(RT):
                        d = nc.vector.bn_stats(e_bn[:, b, r, :], x[:, b, r, :])
                    d.then_inc(E["bn"], 1)
                for b in range(B):
                    dve.wait_ge(E["bn"], b + 1)
                    for r in range(RT):
                        d = nc.vector.bn_aggr(e_mv[:, b, r, :], e_bn[:, b, r, :])
                    d.then_inc(E["mv"], 1)
                for b in range(B):
                    dve.wait_ge(E["mv"], b + 1)
                    nc.vector.tensor_scalar(e_ve[:, b, :], e_mv[:, b, :, 1], EPS2, None, ALU.add).then_inc(E["var"], 1)
                for b in range(B):
                    dve.wait_ge(E["rstd"], b + 1)
                    for r in range(RT):
                        d = nc.vector.tensor_scalar(x[:, b, r, :], x[:, b, r, :], e_mv[:, b, r, 0:1],
                                                    e_rstd[:, b, r:r + 1], ALU.subtract, ALU.mult)
                    d.then_inc(E["z"], 1)
                for b in range(B):
                    dve.wait_ge(E["z"], B + b + 1)
                    for r in range(RT):
                        d = nc.vector.tensor_tensor(x[:, b, r, :], x[:, b, r, :], e_rows[:, 3, :], ALU.mult)
                    d.then_inc(E["zg"], 1)
                for b in range(B):
                    dve.wait_ge(E["zg"], b + 1)
                    for r in range(RT):
                        d = nc.vector.tensor_tensor(x[:, b, r, :], x[:, b, r, :], e_rows[:, 4, :], ALU.add)
                    d.then_inc(E["x"], 1)

        @block.gpsimd
        def _(pool):
            def scale_probs(seg, s, j):
                slot = 2 * (s % 2) + j
                wait_apart(pool, inv_ready, seg.pair(s) * 2 + j + 1, waits_passed)
                for r in range(RT):
                    g = nc.gpsimd.tensor_scalar(probs[:, slot, r, :], probs[:, slot, r, :], row_inv[:, slot, r:r + 1],
                                                1.0, ALU.mult, ALU.mult)
                g.then_inc(probs_ready, 1)

            def normalise(b, n):
                pool.wait_ge(var_ready, n + 1)
                nc.gpsimd.tensor_tensor(rstd[:, :], var_eps[:, :], minus_half[:, :], ALU.pow).then_inc(rstd_ready, 1)
                wait_apart(pool, rstd_ready, n + 1, waits_passed)
                for r in range(RT):
                    g = nc.gpsimd.tensor_scalar(z[:, b, r, :], x[:, b, r, :], mean_var[:, r, 0:1], rstd[:, r:r + 1],
                                                ALU.subtract, ALU.mult)
                g.then_inc(z_ready, 1)

            def split_tn(n_filler, b):
                pool.wait_ge(proj_taken, n_filler + 1)
                nc.gpsimd.tensor_tensor(tn_lo[:, b, :], tnT[:, :], tn_hi[:, b, :].bitcast(F32), ALU.subtract
                                        ).then_inc(tn_ready, 1)

            def add_bias(seg, f):
                kind, b, _ = f
                i = RESIDUAL.index(kind)
                if i == 0:
                    pool.wait_ge(attw_loaded, 16 * ATTW_DMAS * (seg.layer + 1))
                    pool.wait_ge(z_ready, seg.norms_before)
                else:
                    pool.wait_ge(mlp_loaded, 16 * MLP_DMAS * (seg.layer + 1))
                    pool.wait_ge(z_ready, seg.norm_of((RESIDUAL[i - 1], b, 0)) + 1)
                for r in range(RT):
                    g = nc.gpsimd.tensor_tensor(x[:, b, r, :], x[:, b, r, :], rows[:, i, :], ALU.add)
                g.then_inc(bias_added, 1)

            def steps(seg, final=False):
                for s in seg.steps:
                    f = seg.residual_at.get(s)
                    if f:
                        add_bias(seg, f)
                    if not (final and s >= STEPS - 1):
                        scale_probs(seg, s + 1, 0)
                        scale_probs(seg, s + 1, 1)
                    if seg.plan.get(s, ("",))[0].startswith("norm"):
                        split_tn(seg.filler(seg.plan[s]), seg.plan[s][1])
                    if f in seg.normed:
                        normalise(f[1], seg.norm_of(f))

            nc.gpsimd.memset(ident[:, :], 0.0).then_inc(ident_zeroed, 1)
            pool.wait_ge(ident_zeroed, 1)
            nc.gpsimd.affine_select(out=ident[:, :], in_=ident[:, :], compare_op=ALU.not_equal, fill=1.0, base=0,
                                    pattern=[[-1, P]], channel_multiplier=1).then_inc(ident_ready, 1)
            pool.wait_ge(half_ready, 1)
            normalise(0, 0)
            split_tn(START.index(("norm_self", 0, 0)), 0)
            for b in range(1, B):
                normalise(b, b)
            seg = warm_segment()
            scale_probs(seg, STEPS, 0)
            scale_probs(seg, STEPS, 1)
            steps(seg)
            with pool.Fori(0, LAYERS - 1) as l:
                steps(body_segment(l))
            steps(last_segment(), final=True)

            pool.wait_ge(e_loaded, 16 * E_DMAS)
            for m, net in enumerate((0, 2)):
                if net == 2:
                    for b in range(B):
                        pool.wait_ge(E["var"], b + 1)
                        nc.gpsimd.tensor_tensor(e_rstd[:, b, :], e_ve[:, b, :], minus_half[:, :], ALU.pow
                                                ).then_inc(E["rstd"], 1)
                for b in range(B):
                    pool.wait_ge(E["xT_ps"], net * B + b + 1)
                    for r in range(RT):
                        g = nc.gpsimd.tensor_tensor(x[:, b, r, :], x[:, b, r, :], e_rows[:, m, :], ALU.add)
                    g.then_inc(E["biased"], 1)


def kernel(**inputs):
    import numpy as np
    import concourse.bacc as bacc
    from concourse.bass_utils import run_bass_kernel_spmd

    a = {k: np.asarray(v) for k, v in inputs.items()}
    data = {"x": a["x"], "ctx": a["ctx_512"], "srcT": a["ctx_512"].transpose(2, 0, 1),
            "mask_self": a["mask_BxSxS_ik0"], "mask_cross": a["mask_Bx1xS2_if1"],
            "sa_qT": a["L0_xattn_sa_q"].transpose(0, 2, 1), "sa_kT": a["L0_xattn_sa_kv"][:, :, :H * D].transpose(0, 2, 1),
            "ca_qT": a["L0_xattn_ca_q"].transpose(0, 2, 1), "ca_kvT": a["L0_xattn_ca_kv"].transpose(0, 2, 1)}
    for n in ("norm_g", "norm_b", "sa_kv", "sa_ow", "sa_ob", "ca_ow", "ca_ob", "ff_w1", "ff_b1", "ff_w2",
              "ff_b2", "pre_g", "pre_b"):
        data[n] = a["L0_xattn_" + n]
    for net, names in (("L1", ("Wq", "bq", "Wk", "bk", "Wv", "bv", "Wo", "bo")),
                       ("L2", ("Wq", "bq", "Wk", "bk", "Wv", "bv", "gamma", "beta")),
                       ("L3", ("Wq", "bq", "Wk", "bk", "Wv", "bv", "Wo", "bo"))):
        for n in names:
            data[net + "_" + n] = a[net + "_xattn_" + n]
    nc = bacc.Bacc("TRN2", target_bir_lowering=False, num_devices=1)
    arrays, t = {}, {}
    for n, arr in data.items():
        arr = np.ascontiguousarray(arr)
        arrays["in_" + n] = arr
        t[n] = nc.dram_tensor("in_" + n, arr.shape, mybir.dt.from_np(arr.dtype), kind="ExternalInput").ap()
    out = nc.dram_tensor("out", (B, S, TD), F32, kind="ExternalOutput").ap()
    decoder_kernel(nc, t, out)
    r = run_bass_kernel_spmd(nc, [arrays], core_ids=[0])
    return r.results[0]["out"]
```

```python
from contextlib import ExitStack

import concourse.bass as bass
from concourse import mybir

F32 = mybir.dt.float32
F32R = mybir.dt.float32r
I32 = mybir.dt.int32
ALU = mybir.AluOpType
ACT = mybir.ActivationFunctionType

B, S, TD, SD = 4, 256, 128, 64
LAYERS, H, D, FF = 6, 16, 64, 512
P = 128
RT = S // P
PAIRS = H // 2
SELF = B * PAIRS
STEPS = 2 * SELF
LEAD = 4
CUT = PAIRS
MASKED = -float(2 ** 100)
EPS, EPS2 = 1e-5, 1e-6
SCALE = D ** -0.5
SCALE1 = TD ** -0.5

RESIDUAL = ("self_out", "cross_out", "mlp_down")
SPLIT = ("fold_q",)


def next_layers(kind, b, c):
    return kind == "norm_self" and b < 2 or kind == "v" and (b == 0 or b == 1 and c < RT)


def body_fillers():
    out = []
    for b in range(B):
        for c in range(2 * RT):
            start = (STEPS if next_layers("v", b, c) else 0) + PAIRS * b + PAIRS // 2 * (c // RT)
            first = {0: 51, 1: 59 if c < RT else CUT, 2: 11, 3: 18}[b]
            out.append(("v", b, c, first, min(start, CUT + STEPS - 1)))
        end = PAIRS * (b + 1) + 1
        out.append(("norm_cross", b, 0, end + 2, end + 3))
        end = SELF + PAIRS * (b + 1) + 1
        out.append(("norm_mlp", b, 0, end + 2, end + 2))
        out += [("mlp_up", b, c, end + 3 + c, end + 3 + c) for c in range(2)]
        out.append(("mlp_down", b, 0, end + 5, end + 5))
        out.append(("norm_self", b, 0) + ((end + 8, end + 8) if b < 2 else (CUT + 6 * (b - 2), PAIRS * b - LEAD - 2)))
    out += [("fold_q", 0, c, 10, 27) for c in range(2)] + [("fold_o", 0, c, 30, 33) for c in range(2)]
    return out


def place(fillers, steps):
    plan, left = {}, list(fillers)
    for s in steps:
        can = [f for f in left if f[3] <= s]
        if can:
            f = min(can, key=lambda x: x[4])
            assert s <= f[4], (s, f)
            left.remove(f)
            plan[s] = f[:3]
    assert not left, left
    return plan


STEP_RANGE = range(CUT, CUT + STEPS)
PLAN = place(body_fillers(), STEP_RANGE)
START = [("norm_self", 0, 0), ("v", 0, 0), ("v", 0, 1)]
WARM_RANGE = range(STEPS, STEPS + CUT)
WARM = {STEPS + i: f for i, f in enumerate(
    [("norm_self", 1, 0), ("v", 0, 2), ("v", 0, 3), ("v", 1, 0), ("v", 1, 1)])}
WARM_NORMS = {STEPS + 2: 2, STEPS + CUT - 1: 3}
LAST = {s: f for s, f in PLAN.items() if not next_layers(*f)}
LAST_RANGE = range(CUT, max(LAST) + 2)
LAST.update(zip([s for s in LAST_RANGE if s > SELF + 1 and s not in LAST],
                [("context", b, net) for net in range(3) for b in range(B)]))
assert len([f for f in LAST.values() if f[0] == "context"]) == 3 * B
OUTS = {PAIRS * (b + 1) + 1 + (SELF if kind == "cross_out" else 0): (kind, b, 0)
        for kind in ("self_out", "cross_out") for b in range(B)}
NORMS = 3 * B
SPLIT_V = 27
SPLIT_QK = {34 + 3 * i: i for i in range(PAIRS)}
SPLIT_UP = 22


class Segment:

    def __init__(self, layer, steps, plan, fillers_before, norms_before, adds_before, turns_before, folds_before):
        self.layer, self.steps, self.plan = layer, steps, plan
        self.order = [plan[s] for s in sorted(plan)]
        self.fillers_before, self.norms_before, self.adds_before = fillers_before, norms_before, adds_before
        self.turns_before, self.folds_before = turns_before, folds_before
        self.residual_at = {} if plan is WARM else {
            **OUTS, **{s + 1: f for s, f in plan.items() if f[0] in RESIDUAL}}
        self.residual = [self.residual_at[s] for s in sorted(self.residual_at)]
        self.normed = [f for f in self.residual if plan is not LAST or f[0] != "mlp_down"]
        self.turns = [f for f in self.order if f[0].startswith("norm")]
        self.folds = [f for f in self.order if f[0] in SPLIT]

    def pair(self, s):
        return self.layer * STEPS + s

    def self_pair(self, s):
        return (self.layer + s // STEPS) * SELF + s % STEPS

    def filler(self, f):
        return self.fillers_before + self.order.index(f)

    def adds(self, f):
        return self.adds_before + self.residual.index(f)

    def norm_of(self, f):
        return self.norms_before + self.normed.index(f)

    def outs(self, f):
        return self.layer * len(OUTS) + [OUTS[s] for s in sorted(OUTS)].index(f)

    def turn(self, f):
        return self.turns_before + self.turns.index(f)

    def fold(self, f):
        return self.folds_before + self.folds.index(f)

    def rows_ready(self, f):
        if self.plan is WARM:
            return f[1] + 1
        if f[0] == "norm_self" and f[1] >= 2:
            return self.norms_before - 3 + f[1]
        source = {"norm_cross": "self_out", "norm_mlp": "cross_out", "norm_self": "mlp_down"}[f[0]]
        return self.norm_of((source, f[1], 0)) + 1

    def count(self, used, s, before, order):
        here = [order.index(f) for step, f in self.plan.items() if f in used and step < s]
        return before + max((i + 1 for i in here), default=0)

    def taken(self, used, s):
        return self.count(used, s, self.fillers_before, self.order)

    def turned(self, used, s):
        return self.count(used, s, self.turns_before, self.turns)


NETS = (("rows", "query", "scores", "turn", "values", "out"),
        ("rows", "query", "scores", "turn", "out", "gain"),
        ("rows", "query", "scores", "turn", "values", "out"))
ROUNDS_FROM, ROUNDS_A_STEP = STEPS + 1, 1
LAG = ROUNDS_A_STEP * (LAST_RANGE[-1] + 1 - ROUNDS_FROM)
CHAIN = [(net, stage) for net in range(3) for stage in NETS[net]]
ROUNDS = [[CHAIN[t - lag] + (b,) for b, lag in ((3, LAG), (0, 0), (1, 0), (2, 0)) if 0 <= t - lag < len(CHAIN)]
          for t in range(len(CHAIN) + LAG)]
L1_L3, L2 = (0, 2), (1,)
SIGNALLED = {"x": [("out", L1_L3), ("gain", L2)]}
for names, stage, nets in ((("rows_ps", "rowsT"), "rows", (0, 1, 2)), (("biased",), "rows", L1_L3),
                           (("query_ps", "query"), "query", (0, 1, 2)),
                           (("scores_ps", "shifted", "exp"), "scores", (0, 1, 2)),
                           (("inv", "norm"), "turn", (0, 1, 2)), (("turned_ps", "turned"), "turn", L1_L3),
                           (("values_ps", "values"), "values", L1_L3), (("out_ps",), "out", (0, 1, 2)),
                           (("sum", "bn", "mv", "var", "rstd", "z"), "out", L2), (("gained",), "gain", L2)):
    for name in names:
        SIGNALLED[name] = [(stage, nets)]


def nth(name, net, b):
    order = [(n, c) for r in ROUNDS for n, stage, c in r if (stage, True) in [
        (of, n in nets) for of, nets in SIGNALLED[name]]]
    return order.index((net, b)) + 1


def behind(s):
    t = (s - ROUNDS_FROM) * ROUNDS_A_STEP
    rounds = [] if t < 0 else ROUNDS[t:] if s == LAST_RANGE[-1] else ROUNDS[t:t + ROUNDS_A_STEP]
    return [e for r in rounds for e in r]


N_BODY, TURNS_BODY, FOLDS_BODY = len(PLAN), NORMS, 2
N_WARM = len(START) + len(WARM)


def warm_segment():
    return Segment(-1, WARM_RANGE, WARM, len(START), B, 0, 1, 0)


def body_segment(layer):
    return Segment(layer, STEP_RANGE, PLAN, layer * N_BODY + N_WARM, layer * NORMS + B, layer * NORMS,
                   layer * TURNS_BODY + 2, layer * FOLDS_BODY)


def last_segment():
    n = LAYERS - 1
    return Segment(n, LAST_RANGE, LAST, n * N_BODY + N_WARM, n * NORMS + B, n * NORMS, n * TURNS_BODY + 2,
                   n * FOLDS_BODY)


def wait(engine, semaphore, n):
    if not isinstance(n, int) or n > 0:
        engine.wait_ge(semaphore, n)


def wait_apart(engine, semaphore, n, passed):
    engine.wait_ge(semaphore, n)
    engine.sem_inc(passed, 1)


def decoder_kernel(nc, t, out):
    ctx = ExitStack()
    with ctx:
        def sb(name, shape, dt=F32):
            return ctx.enter_context(nc.sbuf_tensor(name, shape, dt))

        def sem(name):
            return ctx.enter_context(nc.semaphore(name))

        x = sb("x", [P, B, RT, TD])
        z = sb("z", [P, B, RT, TD])
        tnT = sb("tnT", [P, S])
        tn_hi = sb("tn_hi", [P, B, S], F32R)
        tn_lo = sb("tn_lo", [P, B, S], F32R)
        qk = sb("qk", [P, 4, 2, 2, S], F32R)
        k_lo = sb("k_lo", [P, 4, 2, S], F32R)
        v = sb("v", [P, 2, RT, H * D])
        probs = sb("probs", [P, 4, RT, S])
        probsT = sb("probsT", [P, 4, RT, S])
        attT = sb("attT", [P, 2, S])
        neg_self = sb("neg_self", [P, B, RT, S])
        neg_cross = sb("neg_cross", [P, B, S])
        neg_none = sb("neg_none", [P, S])
        ident = sb("ident", [P, P])
        srcT = sb("srcT", [P, B, S])
        src_hi = sb("src_hi", [P, B, S], F32R)
        src_lo = sb("src_lo", [P, B, S], F32R)
        src = sb("src", [P, B, RT, SD])
        w_qkv = sb("w_qkv", [P, 3, H * D])
        qk_hi = sb("qk_hi", [P, 2, H * D], F32R)
        qk_lo = sb("qk_lo", [P, 2, H * D], F32R)
        v_hi = sb("v_hi", [P, H * D], F32R)
        v_lo = sb("v_lo", [P, H * D], F32R)
        w_o = sb("w_o", [P, PAIRS, TD])
        cw = sb("cw", [P, 4, PAIRS, TD])
        cw_qT, cw_kT, cw_vT, cw_o = (cw[:, i] for i in range(4))
        c_hi = sb("c_hi", [P, PAIRS, 2 * SD], F32R)
        c_lo = sb("c_lo", [P, PAIRS, 2 * SD], F32R)
        fold_o = sb("fold_o", [P, PAIRS, TD])
        w_up = sb("w_up", [P, FF])
        up_hi = sb("up_hi", [P, FF], F32R)
        up_lo = sb("up_lo", [P, FF], F32R)
        w_down = sb("w_down", [P, FF // P, TD])
        b_up = sb("b_up", [P, FF // P])
        upT = sb("upT", [P, FF // P, S])
        rows = sb("rows", [P, 3, TD])
        norm_gb = sb("norm_gb", [P, 2])
        pre_gb = sb("pre_gb", [P, 2])
        min_u = sb("min_u", [P, 4, RT])
        row_sum = sb("row_sum", [P, 4, RT])
        row_inv = sb("row_inv", [P, 4, RT])
        bn = sb("bn", [P, B, RT, 6])
        mean_var = sb("mean_var", [P, B, RT, 2])
        var_eps = sb("var_eps", [P, B, RT])
        rstd = sb("rstd", [P, B, RT])
        minus_half = sb("minus_half", [P, RT])
        e_kT = sb("e_kT", [P, 3 * B, S])
        e_wq = sb("e_wq", [P, 3, TD])
        e_wk = sb("e_wk", [SD, 3, TD])
        e_wv = sb("e_wv", [SD, 3, TD])
        e_wo = sb("e_wo", [P, 2, TD])
        e_bqkv = sb("e_bqkv", [P, 3, 3])
        e_rows = sb("e_rows", [P, 5, TD])
        table_scratch = sb("table_scratch", [P, RT])
        e_min = sb("e_min", [P, B, RT])
        e_sum = sb("e_sum", [P, B, RT])
        e_inv = sb("e_inv", [P, B, RT])
        part = lambda a, lo, n, m: a[:, lo:lo + n * m].rearrange("p (n m) -> p n m", m=m)
        cw_flat = cw[:, :, :, :].rearrange("p a b c -> p (a b c)")
        e_v = part(v[:, :, :, :].rearrange("p a b c -> p (a b c)"), 0, 3 * B * RT, TD)
        qkv_flat = w_qkv[:, :, :].rearrange("p a b -> p (a b)")
        e_probs = part(qkv_flat, 0, B * RT, S)
        e_probsT = part(cw_flat, 0, B * RT, S)
        e_xT = part(cw_flat, 2 * B * S, B, S)
        e_qT = part(cw_flat, 3 * B * S, B, S)
        e_aT = part(qkv_flat, B * RT * S, B, S)

        scores = ctx.enter_context(nc.psum_tensor("scores", [P, 2, RT, S], F32))
        turned = ctx.enter_context(nc.psum_tensor("turned", [P, 2, RT, S], F32))
        att = ctx.enter_context(nc.psum_tensor("att", [P, 512], F32))
        out_ps = ctx.enter_context(nc.psum_tensor("out_ps", [P, 512], F32))
        q_ps = ctx.enter_context(nc.psum_tensor("q_ps", [P, 2, S], F32))
        proj = ctx.enter_context(nc.psum_tensor("proj", [P, 512], F32))
        halves = lambda a: a.rearrange("p (a b) -> p a b", a=RT)
        flat = lambda a: a.rearrange("p a b -> p (a b)")
        start_banks = [flat(turned[:, 0]), att[:, :], out_ps[:, :]]
        e_a = [turned[:, 0], turned[:, 1], halves(att[:, :]), halves(out_ps[:, :])]
        e_b = [scores[:, 0], scores[:, 1], q_ps[:, :, :], halves(proj[:, :])]

        x_loaded, consts_loaded, masks_loaded = sem("x_loaded"), sem("consts_loaded"), sem("masks_loaded")
        ctx_loaded, e_loaded = sem("ctx_loaded"), sem("e_loaded")
        self_loaded, attw_loaded, mlp_loaded = sem("self_loaded"), sem("attw_loaded"), sem("mlp_loaded")
        ident_zeroed, ident_ready = sem("ident_zeroed"), sem("ident_ready")
        cw_zeroed, neg_ready, k_lo_zeroed = sem("cw_zeroed"), sem("neg_ready"), sem("k_lo_zeroed")
        half_ready = sem("half_ready")
        scores_ready, turned_ready, att_ready, proj_ready = (
            sem("scores_ready"), sem("turned_ready"), sem("att_ready"), sem("proj_ready"))
        out_ready, out_taken = sem("out_ready"), sem("out_taken")
        proj_taken = sem("proj_taken")
        q_ready, q_hi_taken, q_taken = sem("q_ready"), sem("q_hi_taken"), sem("q_taken")
        k_doubled = sem("k_doubled")
        qk_hi_ready, qk_split = sem("qk_hi_ready"), sem("qk_split")
        fold_hi_taken = sem("fold_hi_taken")
        tn_hi_ready = sem("tn_hi_ready")
        tn_ready = sem("tn_ready")
        v_hi_ready, v_split, up_hi_ready, up_split = sem("v_hi_ready"), sem("v_split"), sem("up_hi_ready"), sem("up_split")
        src_hi_ready, src_split = sem("src_hi_ready"), sem("src_split")
        shifted = sem("shifted")
        exp_done, inv_ready, probs_ready = sem("exp_done"), sem("inv_ready"), sem("probs_ready")
        turned_taken = [sem("turned0_taken"), sem("turned1_taken")]
        att_taken = sem("att_taken")
        bn_ready, mv_ready, var_ready, rstd_ready, z_ready = (
            sem("bn_ready"), sem("mv_ready"), sem("var_ready"), sem("rstd_ready"), sem("z_ready"))
        bias_added = sem("bias_added")
        waits_passed = sem("waits_passed")
        E = {n: sem("e_" + n) for n in SIGNALLED}
        stored = sem("stored")

        SELF_DMAS, ATTW_DMAS, MLP_DMAS = 2, 8, 7
        pairs = "(c r) m -> r c m"

        def blocks(q, w, kvT, first, size, loaded):
            heads = kvT[first:first + H * D].rearrange("(c h r) m -> h r c m", h=2, r=D)
            for j in range(2):
                q.dma_start(w[j * D:(j + 1) * D, :, j * size:(j + 1) * size], heads[j]).then_inc(loaded, 16)

        def load_self(q, l):
            q.dma_start(w_qkv[:, 0, :], t["sa_q"][l]).then_inc(self_loaded, 16)
            q.dma_start(w_qkv[:, 1:3, :], t["sa_kv"][l].rearrange("r (a m) -> r a m", a=2)).then_inc(self_loaded, 16)

        def load_attw(q, l):
            row = t["sa_ob"][l:l + 1, :] if isinstance(l, int) else t["sa_ob"][bass.ds(l, 1), :]
            q.dma_start(w_o[:, :, :], t["sa_ow"][l].rearrange(pairs, r=P)).then_inc(attw_loaded, 16)
            q.dma_start(rows[:, 0, :], row.partition_broadcast(P)).then_inc(attw_loaded, 16)
            q.dma_start(cw_qT, t["ca_qT"][l].rearrange(pairs, r=P)).then_inc(attw_loaded, 16)
            q.dma_start(cw_o, t["ca_ow"][l].rearrange(pairs, r=P)).then_inc(attw_loaded, 16)
            blocks(q, cw_kT, t["ca_kvT"][l], 0, SD, attw_loaded)
            blocks(q, cw_vT, t["ca_kvT"][l], H * D, SD, attw_loaded)

        def load_mlp(q, l):
            row = (lambda n: t[n][l:l + 1, :]) if isinstance(l, int) else (lambda n: t[n][bass.ds(l, 1), :])
            q.dma_start(w_up[:, :], t["ff_w1"][l]).then_inc(mlp_loaded, 16)
            q.dma_start(w_down[:, :, :], t["ff_w2"][l].rearrange("(c r) m -> r c m", r=P)).then_inc(mlp_loaded, 16)
            q.dma_start(b_up[:, :], row("ff_b1").rearrange("a (c r) -> r (a c)", r=P)).then_inc(mlp_loaded, 16)
            q.dma_start(rows[:, 1, :], row("ca_ob").partition_broadcast(P)).then_inc(mlp_loaded, 16)
            q.dma_start(rows[:, 2, :], row("ff_b2").partition_broadcast(P)).then_inc(mlp_loaded, 16)
            q.dma_start(pre_gb[:, 0:1], row("pre_g").rearrange("a r -> r a")).then_inc(mlp_loaded, 16)
            q.dma_start(pre_gb[:, 1:2], row("pre_b").rearrange("a r -> r a")).then_inc(mlp_loaded, 16)

        ctx.enter_context(nc.allow_non_contiguous_dma("biases and gains onto partitions"))
        block = ctx.enter_context(nc.Block())

        @block.sync
        def _(sp):
            sp.dma_start(x[:, :, :, :], t["x"].rearrange("b (r p) d -> p b r d", p=P)).then_inc(x_loaded, 16)
            col = lambda n: t[n].rearrange("(r a) -> r a", a=1)
            load_self(sp, 0)
            sp.dma_start(norm_gb[:, 0:1], col("norm_g")).then_inc(consts_loaded, 16)
            sp.dma_start(norm_gb[:, 1:2], col("norm_b")).then_inc(consts_loaded, 16)
            sp.dma_start(neg_self[:, :, :, :].bitcast(I32),
                         t["mask_self"].rearrange("b (r p) k -> p b r k", p=P)).then_inc(masks_loaded, 16)
            sp.dma_start(neg_cross[:, :, :].bitcast(I32).rearrange("p b k -> p (b k)"),
                         t["mask_cross"].rearrange("b a k -> a (b k)").partition_broadcast(P)).then_inc(masks_loaded, 16)
            for j in range(2):
                sp.dma_start(srcT[j * SD:(j + 1) * SD, :, :], t["srcT"][:, :, :]).then_inc(ctx_loaded, 16)
            sp.dma_start(src[:, :, :, :], t["ctx"].rearrange("b (r p) d -> p b r d", p=P)).then_inc(ctx_loaded, 16)
            sp.wait_ge(cw_zeroed, 2)
            load_attw(sp, 0)
            load_mlp(sp, 0)
            for n, name in enumerate(("L1", "L2", "L3")):
                sp.dma_start(e_wq[:, n, :], t[name + "_Wq"]).then_inc(e_loaded, 16)
                sp.dma_start(e_wk[:, n, :], t[name + "_Wk"]).then_inc(e_loaded, 16)
                sp.dma_start(e_wv[:, n, :], t[name + "_Wv"]).then_inc(e_loaded, 16)
                for i, bias in enumerate(("_bq", "_bk", "_bv")):
                    sp.dma_start(e_bqkv[:, n, i:i + 1], col(name + bias)).then_inc(e_loaded, 16)
            sp.dma_start(e_wo[:, 0, :], t["L1_Wo"]).then_inc(e_loaded, 16)
            sp.dma_start(e_wo[:, 1, :], t["L3_Wo"]).then_inc(e_loaded, 16)
            for i, name in enumerate(("L1_bo", "L3_bo", "L2_bv", "L2_gamma", "L2_beta")):
                sp.dma_start(e_rows[:, i, :], t[name].rearrange("(a n) -> a n", a=1).partition_broadcast(P)
                             ).then_inc(e_loaded, 16)
            with sp.Fori(0, LAYERS - 1) as l:
                seg = body_segment(l)
                wait_apart(sp, scores_ready, 2 * seg.pair(10), waits_passed)
                load_self(sp, l + 1)
                wait_apart(sp, scores_ready, 2 * seg.pair(41), waits_passed)
                wait_apart(sp, bias_added, seg.adds_before + B, waits_passed)
                load_attw(sp, l + 1)
                wait_apart(sp, scores_ready, 2 * seg.pair(73), waits_passed)
                wait_apart(sp, bias_added, seg.adds_before + NORMS, waits_passed)
                load_mlp(sp, l + 1)
            for b in range(B):
                sp.wait_ge(E["x"], nth("x", 2, b))
                sp.dma_start(out[b].rearrange("(r p) d -> p r d", p=P), x[:, b]).then_inc(stored, 16)
            sp.wait_ge(stored, 16 * B)

        E_DMAS = 3 * 6 + 2 + 5

        @block.tensor
        def _(pe):
            def head_scores(seg, s, j):
                layer_s = s % STEPS
                cross, b, c = layer_s >= SELF, layer_s % SELF // PAIRS, layer_s % PAIRS
                if j == 0:
                    pe.wait_ge(q_taken, seg.pair(s) + 1)
                    if not cross:
                        pe.wait_ge(k_doubled, seg.self_pair(s) + 1)
                wait(pe, exp_done, (seg.pair(s) - 1) * 2 + j + 1)
                keys = (src_hi[:, b, :], src_lo[:, b, :]) if cross else (qk[:, s % 4, 1, j, :], k_lo[:, s % 4, j, :])
                for r in range(RT):
                    for i, k in enumerate(keys):
                        mm = nc.tensor.matmul(scores[:, j, r, :], qk[:, s % 4, 0, j, r * P:(r + 1) * P], k,
                                              start=(i == 0), stop=(i == 1))
                mm.then_inc(scores_ready, 1)

            def queries(seg, s, waited=False):
                layer_s = s % STEPS
                cross, b, c = layer_s >= SELF, layer_s % SELF // PAIRS, layer_s % PAIRS
                wait(pe, q_taken, seg.pair(s))
                if c == 0 and not waited:
                    kind = "norm_cross" if cross else "norm_self"
                    pe.wait_ge(tn_ready, seg.turned([(kind, b, 0)], s - LEAD))
                    if cross and b == 0:
                        pe.wait_ge(proj_taken, seg.taken([("fold_q", 0, i) for i in range(2)], s - LEAD))
                if not cross and b == 0 and c % 2 == 0:
                    pe.wait_ge(qk_split, (seg.layer + s // STEPS) * PAIRS + c + 2)
                cols = slice(c * P, (c + 1) * P)
                weights = [(c_hi[:, c, :], c_lo[:, c, :])] if cross else [
                    (qk_hi[:, i, cols], qk_lo[:, i, cols]) for i in range(2)]
                for j, (w_hi, w_lo) in enumerate(weights):
                    for i, (w, tn) in enumerate(((w_hi, tn_hi), (w_hi, tn_lo), (w_lo, tn_hi))):
                        mm = nc.tensor.matmul(q_ps[:, j, :], w, tn[:, b, :], start=(i == 0), stop=(i == 2))
                mm.then_inc(q_ready, 1)

            def pair_turn(seg, s, j):
                pe.wait_ge(probs_ready, seg.pair(s) * 2 + j + 1)
                wait(pe, turned_taken[j], seg.pair(s))
                for k in range(RT):
                    for r in range(RT):
                        mm = nc.tensor.transpose(turned[:, j, k, r * P:(r + 1) * P],
                                                 probs[:, 2 * (s % 2) + j, r, k * P:(k + 1) * P], ident[:, :])
                mm.then_inc(turned_ready, 1)

            def pair_values(seg, s):
                layer_s = s % STEPS
                cross, b, c = layer_s >= SELF, layer_s % SELF // PAIRS, layer_s % PAIRS
                for taken in turned_taken:
                    pe.wait_ge(taken, seg.pair(s) + 1)
                wait(pe, att_taken, seg.pair(s))
                if not cross and c % (PAIRS // 2) == 0:
                    half = c // (PAIRS // 2)
                    pe.wait_ge(proj_taken, seg.taken([("v", b, half * RT + i) for i in range(RT)], s + 1))
                for k in range(RT):
                    for j in (0, 1) if k == 0 else (1, 0):
                        val = src[:, b, k, :] if cross else v[:, b % 2, k, (2 * c + j) * D:(2 * c + j + 1) * D]
                        mm = nc.tensor.matmul(att[j * D:(j + 1) * D, 0:S], val, probsT[:, 2 * (s % 2) + j, k, :],
                                              start=(k == 0), stop=(k == RT - 1))
                mm.then_inc(att_ready, 1)

            def output(seg, s):
                layer_s = s % STEPS
                cross, c = layer_s >= SELF, layer_s % PAIRS
                pe.wait_ge(att_taken, seg.pair(s) + 1)
                if c == 0:
                    wait(pe, out_taken, seg.layer * len(OUTS) + s // PAIRS)
                    if not cross:
                        pe.wait_ge(attw_loaded, 16 * ATTW_DMAS * (seg.layer + s // STEPS + 1))
                w = fold_o if cross else w_o
                for r in range(RT):
                    mm = nc.tensor.matmul(out_ps[:, r * P:(r + 1) * P], attT[:, s % 2, r * P:(r + 1) * P], w[:, c, :],
                                          start=(c == 0 and r == 0), stop=(c == PAIRS - 1 and r == RT - 1))
                if c == PAIRS - 1:
                    mm.then_inc(out_ready, 1)

            def filler(seg, f, weights, bank=None):
                kind, b, c = f
                if bank is None:
                    bank = proj[:, :]
                    wait(pe, proj_taken, seg.filler(f))
                if kind in ("norm_self", "norm_cross", "norm_mlp"):
                    pe.wait_ge(z_ready, weights)
                    for r in range(RT):
                        mm = nc.tensor.transpose(bank[:, r * P:(r + 1) * P], z[:, b, r, :], ident[:, :])
                elif kind == "v":
                    half, r = c // RT, c % RT
                    if weights is not None:
                        pe.wait_ge(v_split, weights[0])
                        pe.wait_ge(tn_ready, weights[1])
                    rows_at, cols = slice(r * P, (r + 1) * P), slice(half * 512, (half + 1) * 512)
                    for i, (tn, w) in enumerate(((tn_hi, v_hi), (tn_hi, v_lo), (tn_lo, v_hi))):
                        mm = nc.tensor.matmul(bank[:, :], tn[:, b, rows_at], w[:, cols], start=(i == 0), stop=(i == 2))
                elif kind == "fold_q":
                    pe.wait_ge(attw_loaded, weights)
                    for i in range(4):
                        mm = nc.tensor.matmul(bank[:, i * P:(i + 1) * P], cw_qT[:, 4 * c + i, :],
                                              cw_kT[:, 4 * c + i, :], start=True, stop=True)
                elif kind == "fold_o":
                    pe.wait_ge(attw_loaded, weights)
                    for i in range(4):
                        mm = nc.tensor.matmul(bank[:, i * P:(i + 1) * P], cw_vT[:, 4 * c + i, :],
                                              cw_o[:, 4 * c + i, :], start=True, stop=True)
                elif kind == "context":
                    if weights:
                        pe.wait_ge(e_loaded, weights)
                    nc.tensor.matmul(bank[:, 0:S], e_wk[:, c, :], srcT[0:SD, b, :], start=True, stop=True)
                    for r in range(RT):
                        mm = nc.tensor.matmul(bank[:, S + r * P:S + (r + 1) * P], srcT[0:SD, b, r * P:(r + 1) * P],
                                              e_wv[:, c, :], start=True, stop=True)
                elif kind == "mlp_up":
                    pe.wait_ge(up_split, weights[0])
                    pe.wait_ge(tn_ready, weights[1])
                    for j in range(2):
                        cols = slice((2 * c + j) * P, (2 * c + j + 1) * P)
                        for i, (w, tn) in enumerate(((up_hi, tn_hi), (up_hi, tn_lo), (up_lo, tn_hi))):
                            mm = nc.tensor.matmul(bank[:, j * S:(j + 1) * S], w[:, cols], tn[:, b, :],
                                                  start=(i == 0), stop=(i == 2))
                elif kind == "mlp_down":
                    for r in range(RT):
                        for i in range(FF // P):
                            mm = nc.tensor.matmul(bank[:, r * P:(r + 1) * P], upT[:, i, r * P:(r + 1) * P],
                                                  w_down[:, i, :], start=(i == 0), stop=(i == FF // P - 1))
                mm.then_inc(proj_ready, 1)

            def weights_of(seg, s, f):
                kind, b, c = f
                if kind.startswith("norm"):
                    return seg.rows_ready(f)
                if kind == "v":
                    return (seg.layer + (2 if next_layers(*f) else 1), seg.turned([("norm_self", b, 0)], s)) if c == 0 else None
                if kind == "context":
                    return 16 * E_DMAS if b == c == 0 else None
                if kind.startswith("fold"):
                    return 16 * ATTW_DMAS * (seg.layer + 1)
                if kind == "mlp_up":
                    return seg.layer + 1, seg.turned([("norm_mlp", b, 0)], s)
                return None

            def stage(net, name, b):
                if name == "rows":
                    if net:
                        pe.wait_ge(E["x"], nth("x", net - 1, b))
                    else:
                        pe.wait_ge(proj_taken, last_segment().filler(("mlp_down", b, 0)) + 1)
                    for r in range(RT):
                        mm = nc.tensor.transpose(e_a[b][:, 0, r * P:(r + 1) * P], x[:, b, r, :], ident[:, :])
                    mm.then_inc(E["rows_ps"], 1)
                elif name == "query":
                    pe.wait_ge(E["rowsT"], nth("rowsT", net, b))
                    nc.tensor.matmul(e_a[b][:, 0, :], e_wq[:, net, :], e_xT[:, b, :], start=True, stop=True
                                     ).then_inc(E["query_ps"], 1)
                elif name == "scores":
                    pe.wait_ge(E["query"], nth("query", net, b))
                    for r in range(RT):
                        at = slice(r * P, (r + 1) * P)
                        lhs, rhs = (e_kT[:, B + b, at], e_qT[:, b, :]) if net == 1 else (
                            e_qT[:, b, at], e_kT[:, net * B + b, :])
                        mm = nc.tensor.matmul(e_b[b][:, r, :], lhs, rhs, start=True, stop=True)
                    mm.then_inc(E["scores_ps"], 1)
                elif name == "turn" and net != 1:
                    pe.wait_ge(E["norm"], nth("norm", net, b))
                    for k in range(RT):
                        for r in range(RT):
                            mm = nc.tensor.transpose(e_a[b][:, k, r * P:(r + 1) * P],
                                                     e_probs[:, b * RT + r, k * P:(k + 1) * P], ident[:, :])
                    mm.then_inc(E["turned_ps"], 1)
                elif name == "values":
                    pe.wait_ge(E["turned"], nth("turned", net, b))
                    for k in range(RT):
                        mm = nc.tensor.matmul(e_b[b][:, 0, :], e_v[:, (net * B + b) * RT + k, :],
                                              e_probsT[:, b * RT + k, :], start=(k == 0), stop=(k == RT - 1))
                    mm.then_inc(E["values_ps"], 1)
                elif name == "out" and net == 1:
                    pe.wait_ge(E["norm"], nth("norm", net, b))
                    for r in range(RT):
                        for k in range(RT):
                            mm = nc.tensor.matmul(e_a[b][:, 0, r * P:(r + 1) * P],
                                                  e_probs[:, b * RT + k, r * P:(r + 1) * P],
                                                  e_v[:, (B + b) * RT + k, :], start=(k == 0), stop=(k == RT - 1))
                    mm.then_inc(E["out_ps"], 1)
                elif name == "out":
                    pe.wait_ge(E["values"], nth("values", net, b))
                    for r in range(RT):
                        mm = nc.tensor.matmul(e_a[b][:, 0, r * P:(r + 1) * P], e_aT[:, b, r * P:(r + 1) * P],
                                              e_wo[:, net // 2, :], start=True, stop=True)
                    mm.then_inc(E["out_ps"], 1)

            def steps(seg, final=False):
                for s in seg.steps:
                    if not (final and s >= STEPS - 1):
                        head_scores(seg, s + 1, 0)
                        head_scores(seg, s + 1, 1)
                    if not (final and s >= STEPS - LEAD):
                        queries(seg, s + LEAD)
                    if not (final and s > STEPS + 1) and not (seg.plan is WARM and s < STEPS + 2):
                        output(seg, s - 2)
                    if not (final and s >= STEPS):
                        pair_turn(seg, s, 0)
                        pair_turn(seg, s, 1)
                    if s in seg.plan:
                        filler(seg, seg.plan[s], weights_of(seg, s, seg.plan[s]))
                    if not (final and s > STEPS) and not (seg.plan is WARM and s == STEPS):
                        pair_values(seg, s - 1)
                    for e in behind(s) if final else []:
                        stage(*e)

            pe.wait_ge(ident_ready, 1)
            first = warm_segment()
            filler(None, START[0], 1, start_banks[0])
            pe.wait_ge(tn_ready, 1)
            queries(first, STEPS, waited=True)
            queries(first, STEPS + 1)
            pe.wait_ge(k_lo_zeroed, 1)
            head_scores(first, STEPS, 0)
            head_scores(first, STEPS, 1)
            queries(first, STEPS + 2)
            queries(first, STEPS + 3)
            for n, f in enumerate(START[1:]):
                filler(None, f, (1, 1) if n == 0 else None, start_banks[1 + n])
            steps(first)
            pe.wait_ge(ctx_loaded, 16 * 3)
            pe.wait_ge(src_split, 1)
            with pe.Fori(0, LAYERS - 1) as l:
                steps(body_segment(l))
            steps(last_segment(), final=True)

        @block.scalar
        def _(act):
            def exps(seg, s, j):
                act.wait_ge(shifted, seg.pair(s) * 2 + j + 1)
                slot = 2 * (s % 2) + j
                for r in range(RT):
                    e = nc.scalar.activation(probs[:, slot, r, :], scores[:, j, r, :], ACT.Exp,
                                             bias=min_u[:, slot, r:r + 1], scale=-1.0,
                                             accum_out=row_sum[:, slot, r:r + 1])
                e.then_inc(exp_done, 1)

            def take_turned(seg, s):
                act.wait_ge(turned_ready, (seg.pair(s) + 1) * 2)
                nc.scalar.activation(probsT[:, 2 * (s % 2) + 1, :, :], turned[:, 1, :, :], ACT.Copy
                                     ).then_inc(turned_taken[1], 1)

            def take_att(seg, s):
                act.wait_ge(att_ready, seg.pair(s) + 1)
                nc.scalar.activation(attT[:, s % 2, :], att[:, 0:S], ACT.Copy).then_inc(att_taken, 1)

            def take_q(seg, s):
                act.wait_ge(q_ready, seg.pair(s) + 1)
                n = 1 if s % STEPS >= SELF else 2
                for j in range(2):
                    a = nc.scalar.activation(qk[0:SD, s % 4, 0:n, j, :], q_ps[j * SD:(j + 1) * SD, 0:n, :], ACT.Copy)
                a.then_inc(q_hi_taken, 1)

            def take(n, f, layer, bank=proj[:, :]):
                kind, b, c = f
                act.wait_ge(proj_ready, n + 1)
                quarters = bank[:, :].rearrange("p (a b) -> p a b", a=4)
                if kind.startswith("norm"):
                    if kind == "norm_mlp":
                        act.wait_ge(mlp_loaded, 16 * MLP_DMAS * (layer + 1))
                    gb = pre_gb if kind == "norm_mlp" else norm_gb
                    nc.scalar.activation(tnT[:, :], bank[:, 0:S], ACT.Identity, scale=gb[:, 0:1], bias=gb[:, 1:2]
                                         ).then_inc(proj_taken, 1)
                elif kind == "mlp_up":
                    for i in range(2):
                        a = nc.scalar.activation(upT[:, 2 * c + i, :], bank[:, i * S:(i + 1) * S], ACT.Relu,
                                                 bias=b_up[:, 2 * c + i:2 * c + i + 1])
                    a.then_inc(proj_taken, 1)
                elif kind == "fold_q":
                    nc.scalar.activation(c_hi[:, 4 * c:4 * c + 4, :], quarters, ACT.Copy).then_inc(fold_hi_taken, 1)
                elif kind == "context":
                    nc.scalar.activation(e_kT[:, c * B + b, :], bank[:, 0:S], ACT.Identity, bias=e_bqkv[:, c, 1:2])
                    nc.scalar.activation(e_v[:, (c * B + b) * RT:(c * B + b + 1) * RT, :], halves(bank[:, :])[:, 1, :],
                                         ACT.Copy).then_inc(proj_taken, 1)
                elif kind == "fold_o":
                    nc.scalar.activation(fold_o[:, 4 * c:4 * c + 4, :], quarters, ACT.Copy).then_inc(proj_taken, 1)

            def stage(net, name, b):
                if name == "rows":
                    act.wait_ge(E["rows_ps"], nth("rows_ps", net, b))
                    nc.scalar.activation(e_xT[:, b, :], e_a[b][:, 0, :], ACT.Copy).then_inc(E["rowsT"], 1)
                elif name == "query":
                    act.wait_ge(E["query_ps"], nth("query_ps", net, b))
                    nc.scalar.activation(e_qT[:, b, :], e_a[b][:, 0, :], ACT.Identity, bias=e_bqkv[:, net, 0:1]
                                         ).then_inc(E["query"], 1)
                elif name == "scores":
                    act.wait_ge(E["shifted"], nth("shifted", net, b))
                    for r in range(RT):
                        e = nc.scalar.activation(e_probs[:, b * RT + r, :], e_b[b][:, r, :], ACT.Exp,
                                                 bias=e_min[:, b, r:r + 1], scale=-1.0, accum_out=e_sum[:, b, r:r + 1])
                    e.then_inc(E["exp"], 1)
                elif name == "turn" and net != 1:
                    act.wait_ge(E["turned_ps"], nth("turned_ps", net, b))
                    nc.scalar.activation(e_probsT[:, b * RT:(b + 1) * RT, :], e_a[b], ACT.Copy).then_inc(E["turned"], 1)
                elif name == "values":
                    act.wait_ge(E["values_ps"], nth("values_ps", net, b))
                    nc.scalar.activation(e_aT[:, b, :], e_b[b][:, 0, :], ACT.Identity, bias=e_bqkv[:, net, 2:3]
                                         ).then_inc(E["values"], 1)

            def steps(seg, final=False):
                for s in seg.steps:
                    if s > seg.steps[0] and not (final and s > STEPS + 1) and not (seg.plan is WARM and s == STEPS + 1):
                        take_att(seg, s - 2)
                    heads = not (final and s >= STEPS - 1)
                    if heads:
                        exps(seg, s + 1, 0)
                    if not (final and s >= STEPS - LEAD):
                        take_q(seg, s + LEAD)
                    if heads:
                        exps(seg, s + 1, 1)
                    if not (final and s >= STEPS):
                        take_turned(seg, s)
                    if s in seg.plan and seg.plan[s][0] not in RESIDUAL + ("v",):
                        take(seg.filler(seg.plan[s]), seg.plan[s], seg.layer)
                    for e in behind(s) if final else []:
                        stage(*e)
                if not final:
                    take_att(seg, seg.steps[-1] - 1)

            act.wait_ge(half_ready, 1)
            nc.scalar.activation(table_scratch[:, :], minus_half[:, :], ACT.Exp)
            seg = warm_segment()
            act.wait_ge(consts_loaded, 32)
            take(0, START[0], 0, start_banks[0])
            take_q(seg, STEPS)
            take_q(seg, STEPS + 1)
            exps(seg, STEPS, 0)
            exps(seg, STEPS, 1)
            take_q(seg, STEPS + 2)
            take_q(seg, STEPS + 3)
            steps(seg)
            with act.Fori(0, LAYERS - 1) as l:
                steps(body_segment(l))
            steps(last_segment(), final=True)

        @block.vector
        def _(dve):
            def shift(seg, s, j):
                layer_s = s % STEPS
                cross, b = layer_s >= SELF, layer_s % SELF // PAIRS
                slot = 2 * (s % 2) + j
                wait_apart(dve, scores_ready, seg.pair(s) * 2 + j + 1, waits_passed)
                for r in range(RT):
                    d = nc.vector.tensor_tensor_reduce(
                        out=scores[:, j, r, :], in0=scores[:, j, r, :],
                        in1=neg_cross[:, b, :] if cross else neg_self[:, b, r, :], scale=-SCALE, scalar=3e38,
                        op0=ALU.add, op1=ALU.min, accum_out=min_u[:, slot, r:r + 1])
                d.then_inc(shifted, 1)

            def invert(seg, s, j):
                slot = 2 * (s % 2) + j
                dve.wait_ge(exp_done, seg.pair(s) * 2 + j + 1)
                nc.vector.reciprocal(row_inv[:, slot, :], row_sum[:, slot, :]).then_inc(inv_ready, 1)

            def take_turned(seg, s):
                dve.wait_ge(turned_ready, seg.pair(s) * 2 + 1)
                nc.vector.tensor_copy(probsT[:, 2 * (s % 2), :, :], turned[:, 0, :, :]).then_inc(turned_taken[0], 1)

            def take_q(seg, s):
                dve.wait_ge(q_hi_taken, seg.pair(s) + 1)
                for i in range(1 if s % STEPS >= SELF else 2):
                    for j in range(2):
                        lo = k_lo[0:SD, s % 4, j, :] if i else qk[SD:P, s % 4, 0, j, :]
                        d = nc.vector.tensor_tensor(lo, q_ps[j * SD:(j + 1) * SD, i, :],
                                                    qk[0:SD, s % 4, i, j, :].bitcast(F32), ALU.subtract)
                d.then_inc(q_taken, 1)

            def split_fold(n_fold, f):
                dve.wait_ge(fold_hi_taken, n_fold + 1)
                at = slice(4 * f[2], 4 * f[2] + 4)
                nc.vector.tensor_tensor(c_lo[:, at, :], proj[:, :].rearrange("p (a b) -> p a b", a=4),
                                        c_hi[:, at, :].bitcast(F32), ALU.subtract).then_inc(proj_taken, 1)

            def split(whole, hi, lo, hi_ready, ready, n):
                nc.vector.tensor_copy(hi, whole).then_inc(hi_ready, 1)
                dve.wait_ge(hi_ready, n + 1)
                d = nc.vector.tensor_tensor(lo, whole, hi.bitcast(F32), ALU.subtract)
                if ready is not None:
                    d.then_inc(ready, 1)

            def split_v(part, layer):
                if part == 0:
                    dve.wait_ge(self_loaded, 16 * SELF_DMAS * (layer + 1))
                at = slice(part * 256, (part + 1) * 256)
                split(w_qkv[:, 2, at], v_hi[:, at], v_lo[:, at], v_hi_ready, v_split if part == 3 else None, 4 * layer + part)

            def split_qk(part, layer):
                if part == 0:
                    dve.wait_ge(self_loaded, 16 * SELF_DMAS * (layer + 1))
                i, at = part % 2, slice(part // 2 * 256, (part // 2 + 1) * 256)
                split(w_qkv[:, i, at], qk_hi[:, i, at], qk_lo[:, i, at], qk_hi_ready, qk_split, PAIRS * layer + part)

            def split_up(part, layer):
                if part == 0:
                    dve.wait_ge(mlp_loaded, 16 * MLP_DMAS * (layer + 1))
                at = slice(part * 256, (part + 1) * 256)
                split(w_up[:, at], up_hi[:, at], up_lo[:, at], up_hi_ready, up_split if part == 1 else None,
                      2 * layer + part)

            def take_v(n, f, bank=proj[:, :]):
                _, b, c = f
                dve.wait_ge(proj_ready, n + 1)
                nc.vector.tensor_copy(v[:, b % 2, c % RT, (c // RT) * 512:(c // RT + 1) * 512], bank
                                      ).then_inc(proj_taken, 1)

            def stats(b, n):
                moments(b)
                aggregate(b, n)
                add_eps(b, n)

            def moments(b):
                for r in range(RT):
                    d = nc.vector.bn_stats(bn[:, b, r, :], x[:, b, r, :])
                d.then_inc(bn_ready, 1)

            def aggregate(b, n):
                wait_apart(dve, bn_ready, n + 1, waits_passed)
                for r in range(RT):
                    d = nc.vector.bn_aggr(mean_var[:, b, r, :], bn[:, b, r, :])
                d.then_inc(mv_ready, 1)

            def add_eps(b, n):
                dve.wait_ge(mv_ready, n + 1)
                nc.vector.tensor_scalar(var_eps[:, b, :], mean_var[:, b, :, 1], EPS, None, ALU.add).then_inc(var_ready, 1)

            def normalise(b, n):
                dve.wait_ge(rstd_ready, n + 1)
                for r in range(RT):
                    d = nc.vector.tensor_scalar(z[:, b, r, :], x[:, b, r, :], mean_var[:, b, r, 0:1],
                                                rstd[:, b, r:r + 1], ALU.subtract, ALU.mult)
                d.then_inc(z_ready, 1)

            def add(seg, f):
                if f[0] == "mlp_down":
                    ready, taken, n, bank = proj_ready, proj_taken, seg.filler(f), proj
                else:
                    ready, taken, n, bank = out_ready, out_taken, seg.outs(f), out_ps
                dve.wait_ge(ready, n + 1)
                dve.wait_ge(bias_added, seg.adds(f) + 1)
                nc.vector.tensor_tensor(x[:, f[1]], halves(bank[:, 0:S]), x[:, f[1]], ALU.add).then_inc(taken, 1)
                return taken, n + 1

            def stage(net, name, b):
                if name == "rows" and net == 1:
                    dve.wait_ge(proj_taken, last_segment().filler(("context", b, net)) + 1)
                    for r in range(RT):
                        at = (B + b) * RT + r
                        nc.vector.tensor_tensor(e_v[:, at, :], e_v[:, at, :], e_rows[:, 2, :], ALU.add)
                elif name == "scores":
                    dve.wait_ge(E["scores_ps"], nth("scores_ps", net, b))
                    for r in range(RT):
                        d = nc.vector.tensor_tensor_reduce(
                            out=e_b[b][:, r, :], in0=e_b[b][:, r, :], in1=neg_none[:, :], scale=-SCALE1, scalar=3e38,
                            op0=ALU.add, op1=ALU.min, accum_out=e_min[:, b, r:r + 1])
                    d.then_inc(E["shifted"], 1)
                elif name == "turn":
                    dve.wait_ge(E["exp"], nth("exp", net, b))
                    nc.vector.reciprocal(e_inv[:, b, :], e_sum[:, b, :]).then_inc(E["inv"], 1)
                    dve.wait_ge(E["inv"], nth("inv", net, b))
                    for r in range(RT):
                        d = nc.vector.tensor_scalar(e_probs[:, b * RT + r, :], e_probs[:, b * RT + r, :],
                                                    e_inv[:, b, r:r + 1], None, ALU.mult)
                    d.then_inc(E["norm"], 1)
                elif name == "out":
                    dve.wait_ge(E["out_ps"], nth("out_ps", net, b))
                    if net != 1:
                        dve.wait_ge(E["biased"], nth("biased", net, b))
                    nc.vector.tensor_tensor(x[:, b], halves(e_a[b][:, 0, :]), x[:, b], ALU.add
                                            ).then_inc(E["sum"] if net == 1 else E["x"], 1)
                    if net == 1:
                        dve.wait_ge(E["sum"], nth("sum", net, b))
                        for r in range(RT):
                            d = nc.vector.bn_stats(bn[:, b, r, :], x[:, b, r, :])
                        d.then_inc(E["bn"], 1)
                        dve.wait_ge(E["bn"], nth("bn", net, b))
                        for r in range(RT):
                            d = nc.vector.bn_aggr(mean_var[:, b, r, :], bn[:, b, r, :])
                        d.then_inc(E["mv"], 1)
                        dve.wait_ge(E["mv"], nth("mv", net, b))
                        nc.vector.tensor_scalar(var_eps[:, b, :], mean_var[:, b, :, 1], EPS2, None, ALU.add
                                                ).then_inc(E["var"], 1)
                elif name == "gain":
                    dve.wait_ge(E["z"], nth("z", net, b))
                    for r in range(RT):
                        d = nc.vector.tensor_tensor(x[:, b, r, :], z[:, b, r, :], e_rows[:, 3, :], ALU.mult)
                    d.then_inc(E["gained"], 1)
                    dve.wait_ge(E["gained"], nth("gained", net, b))
                    for r in range(RT):
                        d = nc.vector.tensor_tensor(x[:, b, r, :], x[:, b, r, :], e_rows[:, 4, :], ALU.add)
                    d.then_inc(E["x"], 1)

            def steps(seg, final=False):
                for s in seg.steps:
                    heads = not (final and s >= STEPS - 1)
                    turns = not (final and s >= STEPS)
                    if heads:
                        shift(seg, s + 1, 0)
                        shift(seg, s + 1, 1)
                    before = seg.plan.get(s - 1, ("",))
                    if before[0] in SPLIT:
                        split_fold(seg.fold(before), before)
                    if before[0] == "v":
                        take_v(seg.filler(before), before)
                    f = seg.residual_at.get(s - 1)
                    if s == CUT:
                        normalise(B - 1, seg.norms_before - 1)
                    elif f in seg.normed:
                        normalise(f[1], seg.norm_of(f))
                    f = seg.residual_at.get(s)
                    if f:
                        summed = add(seg, f)
                    normed = f in seg.normed
                    if heads:
                        invert(seg, s + 1, 0)
                    if turns:
                        take_turned(seg, s)
                    if normed:
                        dve.wait_ge(*summed)
                        moments(f[1])
                    if not (final and s >= STEPS - LEAD):
                        take_q(seg, s + LEAD)
                    if normed:
                        aggregate(f[1], seg.norm_of(f))
                    if heads:
                        invert(seg, s + 1, 1)
                    if normed:
                        add_eps(f[1], seg.norm_of(f))
                    if seg.plan is PLAN and s - SPLIT_V in range(4):
                        split_v(s - SPLIT_V, seg.layer + 1)
                    if seg.plan is PLAN and s in SPLIT_QK:
                        split_qk(SPLIT_QK[s], seg.layer + 1)
                    if seg.plan is WARM and s in WARM_NORMS:
                        stats(WARM_NORMS[s], WARM_NORMS[s])
                        if s < seg.steps[-1]:
                            normalise(WARM_NORMS[s], WARM_NORMS[s])
                    if s - SPLIT_UP in range(2):
                        split_up(s - SPLIT_UP, seg.layer)
                    for e in behind(s) if final else []:
                        stage(*e)

            nc.vector.memset(minus_half[:, :], -0.5).then_inc(half_ready, 1)
            dve.wait_ge(x_loaded, 16)
            stats(0, 0)
            normalise(0, 0)
            seg = warm_segment()
            for part in range(4):
                split_qk(part, 0)
            dve.wait_ge(neg_ready, 1)
            for i in range(4):
                d = nc.vector.tensor_copy(k_lo[SD:P, i, :, :], neg_none[SD:P, :].unsqueeze(1).to_broadcast([SD, 2, S]))
            d.then_inc(k_lo_zeroed, 1)
            take_q(seg, STEPS)
            take_q(seg, STEPS + 1)
            dve.wait_ge(masks_loaded, 32)
            for m in (neg_self[:, :, :, :].rearrange("p a b c -> p (a b c)"), neg_cross[:, :, :].rearrange("p a b -> p (a b)")):
                nc.vector.tensor_scalar(m, m.bitcast(I32), 0, MASKED, ALU.is_equal, ALU.mult).then_inc(neg_ready, 1)
            dve.wait_ge(neg_ready, 3)
            for j in range(2):
                shift(seg, STEPS, j)
            take_q(seg, STEPS + 2)
            take_q(seg, STEPS + 3)
            for j in range(2):
                invert(seg, STEPS, j)
            for part in range(4, PAIRS):
                split_qk(part, 0)
            for i in range(4):
                split_v(i, 0)
            for n in (1, 2):
                take_v(n, START[n], start_banks[n])
            stats(1, 1)
            normalise(1, 1)
            dve.wait_ge(ctx_loaded, 16 * 3)
            split(srcT[:, :, :], src_hi[:, :, :], src_lo[:, :, :], src_hi_ready, src_split, 0)
            steps(seg)
            with dve.Fori(0, LAYERS - 1) as l:
                steps(body_segment(l))
            dve.wait_ge(e_loaded, 16 * E_DMAS)
            steps(last_segment(), final=True)

        @block.gpsimd
        def _(pool):
            def scale_probs(seg, s, j):
                slot = 2 * (s % 2) + j
                wait_apart(pool, inv_ready, seg.pair(s) * 2 + j + 1, waits_passed)
                for r in range(RT):
                    g = nc.gpsimd.tensor_scalar(probs[:, slot, r, :], probs[:, slot, r, :], row_inv[:, slot, r:r + 1],
                                                1.0, ALU.mult, ALU.mult)
                g.then_inc(probs_ready, 1)

            def double(seg, s, in_front):
                last, n = in_front
                wait_apart(pool, last, n, waits_passed)
                wait_apart(pool, q_hi_taken, seg.pair(s) + 1, waits_passed)
                nc.gpsimd.tensor_scalar(qk[SD:P, s % 4, 1, :, :], qk[0:SD, s % 4, 1, :, :].bitcast(F32), 1.0, 1.0,
                                        ALU.mult, ALU.mult).then_inc(k_doubled, 1)
                wait_apart(pool, k_doubled, seg.self_pair(s) + 1, waits_passed)

            def root(b, n):
                pool.wait_ge(var_ready, n + 1)
                nc.gpsimd.tensor_tensor(rstd[:, b, :], var_eps[:, b, :], minus_half[:, :], ALU.pow
                                        ).then_inc(rstd_ready, 1)

            def split_tn(n_filler, b, n):
                wait_apart(pool, proj_taken, n_filler + 1, waits_passed)
                nc.gpsimd.tensor_scalar(tn_hi[:, b, :], tnT[:, :], 1.0, 1.0, ALU.mult, ALU.mult).then_inc(tn_hi_ready, 1)
                pool.wait_ge(tn_hi_ready, n + 1)
                nc.gpsimd.tensor_tensor(tn_lo[:, b, :], tnT[:, :], tn_hi[:, b, :].bitcast(F32), ALU.subtract
                                        ).then_inc(tn_ready, 1)

            def add_bias(seg, f):
                kind, b, _ = f
                i = RESIDUAL.index(kind)
                if i == 0:
                    pool.wait_ge(attw_loaded, 16 * ATTW_DMAS * (seg.layer + 1))
                    pool.wait_ge(z_ready, seg.norms_before - (0 if b == B - 1 else 1))
                else:
                    pool.wait_ge(mlp_loaded, 16 * MLP_DMAS * (seg.layer + 1))
                    pool.wait_ge(z_ready, seg.norm_of((RESIDUAL[i - 1], b, 0)) + 1)
                for r in range(RT):
                    g = nc.gpsimd.tensor_tensor(x[:, b, r, :], x[:, b, r, :], rows[:, i, :], ALU.add)
                g.then_inc(bias_added, 1)

            def stage(net, name, b):
                if name == "rows" and net != 1:
                    pool.wait_ge(E["rows_ps"], nth("rows_ps", net, b))
                    for r in range(RT):
                        g = nc.gpsimd.tensor_tensor(x[:, b, r, :], x[:, b, r, :], e_rows[:, net // 2, :], ALU.add)
                    g.then_inc(E["biased"], 1)
                elif name == "out" and net == 1:
                    pool.wait_ge(E["var"], nth("var", net, b))
                    nc.gpsimd.tensor_tensor(rstd[:, b, :], var_eps[:, b, :], minus_half[:, :], ALU.pow
                                            ).then_inc(E["rstd"], 1)
                    pool.wait_ge(E["rstd"], nth("rstd", net, b))
                    for r in range(RT):
                        g = nc.gpsimd.tensor_scalar(z[:, b, r, :], x[:, b, r, :], mean_var[:, b, r, 0:1],
                                                    rstd[:, b, r:r + 1], ALU.subtract, ALU.mult)
                    g.then_inc(E["z"], 1)

            def steps(seg, final=False):
                for s in seg.steps:
                    if s + 1 in seg.residual_at:
                        add_bias(seg, seg.residual_at[s + 1])
                    f = seg.residual_at.get(s)
                    if not (final and s >= STEPS - 1):
                        scale_probs(seg, s + 1, 0)
                    if (s + LEAD) % STEPS < SELF and not (final and s >= STEPS - LEAD):
                        double(seg, s + LEAD, (probs_ready, seg.pair(s + 1) * 2 + 1))
                    if not (final and s >= STEPS - 1):
                        scale_probs(seg, s + 1, 1)
                    if f in seg.normed:
                        root(f[1], seg.norm_of(f))
                    if seg.plan.get(s, ("",))[0].startswith("norm"):
                        split_tn(seg.filler(seg.plan[s]), seg.plan[s][1], seg.turn(seg.plan[s]))
                    if seg.plan is WARM and s in WARM_NORMS:
                        root(WARM_NORMS[s], WARM_NORMS[s])
                    for e in behind(s) if final else []:
                        stage(*e)

            nc.gpsimd.memset(ident[:, :], 0.0).then_inc(ident_zeroed, 1)
            pool.wait_ge(ident_zeroed, 1)
            nc.gpsimd.affine_select(out=ident[:, :], in_=ident[:, :], compare_op=ALU.not_equal, fill=1.0, base=0,
                                    pattern=[[-1, P]], channel_multiplier=1).then_inc(ident_ready, 1)
            for w in (cw_kT, cw_vT):
                nc.gpsimd.memset(w, 0.0).then_inc(cw_zeroed, 1)
            nc.gpsimd.memset(neg_none[:, :], 0.0).then_inc(neg_ready, 1)
            pool.wait_ge(half_ready, 1)
            root(0, 0)
            split_tn(START.index(("norm_self", 0, 0)), 0, 0)
            seg = warm_segment()
            double(seg, STEPS, (tn_ready, 1))
            double(seg, STEPS + 1, (k_doubled, 1))
            scale_probs(seg, STEPS, 0)
            scale_probs(seg, STEPS, 1)
            double(seg, STEPS + 2, (probs_ready, 2))
            double(seg, STEPS + 3, (k_doubled, 3))
            root(1, 1)
            steps(seg)
            with pool.Fori(0, LAYERS - 1) as l:
                steps(body_segment(l))
            pool.wait_ge(e_loaded, 16 * E_DMAS)
            steps(last_segment(), final=True)


def kernel(**inputs):
    import numpy as np
    import concourse.bacc as bacc
    from concourse.bass_utils import run_bass_kernel_spmd

    a = {k: np.asarray(v) for k, v in inputs.items()}
    data = {"x": a["x"], "ctx": a["ctx_512"], "srcT": a["ctx_512"].transpose(2, 0, 1),
            "mask_self": a["mask_BxSxS_ik0"], "mask_cross": a["mask_Bx1xS2_if1"],
            "sa_q": a["L0_xattn_sa_q"],
                        "ca_qT": a["L0_xattn_ca_q"].transpose(0, 2, 1), "ca_kvT": a["L0_xattn_ca_kv"].transpose(0, 2, 1)}
    for n in ("norm_g", "norm_b", "sa_kv", "sa_ow", "sa_ob", "ca_ow", "ca_ob", "ff_w1", "ff_b1", "ff_w2",
              "ff_b2", "pre_g", "pre_b"):
        data[n] = a["L0_xattn_" + n]
    for net, names in (("L1", ("Wq", "bq", "Wk", "bk", "Wv", "bv", "Wo", "bo")),
                       ("L2", ("Wq", "bq", "Wk", "bk", "Wv", "bv", "gamma", "beta")),
                       ("L3", ("Wq", "bq", "Wk", "bk", "Wv", "bv", "Wo", "bo"))):
        for n in names:
            data[net + "_" + n] = a[net + "_xattn_" + n]
    nc = bacc.Bacc("TRN2", target_bir_lowering=False, num_devices=1)
    arrays, t = {}, {}
    for n, arr in data.items():
        arr = np.ascontiguousarray(arr)
        arrays["in_" + n] = arr
        t[n] = nc.dram_tensor("in_" + n, arr.shape, mybir.dt.from_np(arr.dtype), kind="ExternalInput").ap()
    out = nc.dram_tensor("out", (B, S, TD), F32, kind="ExternalOutput").ap()
    decoder_kernel(nc, t, out)
    r = run_bass_kernel_spmd(nc, [arrays], core_ids=[0])
    return r.results[0]["out"]
```
